# Optimizing a Trainium2 kernel written in Bass

```python
import numpy as np
import jax
import jax.numpy as jnp

def _softmax(x, axis=-1):
    return jax.nn.softmax(x, axis=axis)

def _gelu(x):
    return jax.nn.gelu(x, approximate=True)

def _silu(x):
    return jax.nn.silu(x)

def _sigmoid(x):
    return jax.nn.sigmoid(x)

def _layernorm(x, axis=-1, eps=1e-05):
    m = jnp.mean(x, axis=axis, keepdims=True)
    v = jnp.var(x, axis=axis, keepdims=True)
    return (x - m) / jnp.sqrt(v + eps)

def _scatter_add(tgt, idx, src, axis=0):
    return tgt.at[idx].add(src)

def _segment_sum(src, seg, n):
    return jax.ops.segment_sum(src, seg, n)
kernel_name = 'mk_macaron_d1_jaxref_r8_6c8691'

def setup_inputs(seed: int=0):
    np.random.seed(seed)
    _w = jnp.asarray

    def _L0_attn_setup():
        import jax, jax.numpy as jnp
        import numpy as np
        D_MODEL = 128
        N_HEADS = 16
        D_HEAD = D_MODEL // N_HEADS
        WINDOW = 32
        CAUSAL = True
        NEG = -1000000000.0

        def build_sliding_window_mask(seq_len, window_size, causal=True):
            i = jnp.arange(seq_len)[:, None]
            j = jnp.arange(seq_len)[None, :]
            if causal:
                attend = (j <= i) & (j >= i - window_size)
            else:
                half = window_size // 2
                attend = jnp.abs(j - i) <= half
            return jnp.where(attend, 0.0, NEG).astype(jnp.float32)
        key = jax.random.key(seed)
        k0, k1, k2, k3, k4 = jax.random.split(key, 5)
        B, T = (1, 512)
        s = 1.0 / np.sqrt(D_MODEL)
        return {'x': jax.random.normal(k0, (B, T, D_MODEL), dtype=jnp.float32), 'Wq': jax.random.normal(k1, (D_MODEL, D_MODEL), dtype=jnp.float32) * s, 'Wk': jax.random.normal(k2, (D_MODEL, D_MODEL), dtype=jnp.float32) * s, 'Wv': jax.random.normal(k3, (D_MODEL, D_MODEL), dtype=jnp.float32) * s, 'Wo': jax.random.normal(k4, (D_MODEL, D_MODEL), dtype=jnp.float32) * s}
    _L0_attn_in = _L0_attn_setup()

    def _L0_ffn_setup():
        import jax, jax.numpy as jnp
        import numpy as np
        DIM = 128
        DEPTH = 6
        HEADS = 16
        DIM_HEAD = 64
        WINDOW = 32
        INNER = HEADS * DIM_HEAD
        DIM_INNER = int(DIM * 4 * 2 / 3)
        QK_SCALE = 8.0

        def shift_tokens(t):
            a, s = jnp.split(t, 2, -1)
            s = jnp.pad(s, ((0, 0), (1, 0), (0, 0)))[:, :-1]
            return jnp.concatenate([a, s], -1)

        def l2norm(t):
            return t / jnp.maximum(jnp.linalg.norm(t, axis=-1, keepdims=True), 1e-12)

        def rotate_half(x):
            x1, x2 = jnp.split(x, 2, -1)
            return jnp.concatenate([-x2, x1], -1)

        def rotary_tables(n):
            half = jnp.arange(0, DIM_HEAD, 2, dtype=jnp.float32)
            inv_freq = 1.0 / 10000.0 ** (half / DIM_HEAD)
            t = jnp.arange(n, dtype=jnp.float32)
            freqs = t[:, None] * inv_freq[None, :]
            freqs = jnp.concatenate([freqs, freqs], -1)
            base_scale = (half + 0.4 * DIM_HEAD) / (1.4 * DIM_HEAD)
            power = (t - n // 2) / (WINDOW // 2)
            scale = base_scale[None, :] ** power[:, None]
            scale = jnp.concatenate([scale, scale], -1)
            return (freqs, scale)

        def local_attention(q, k, v):
            b, h, n, d = q.shape
            w = WINDOW
            nw = n // w
            bq = q.reshape(b, h, nw, w, d)
            bk = k.reshape(b, h, nw, w, d)
            bv = v.reshape(b, h, nw, w, d)

            def look(t):
                p = jnp.pad(t, ((0, 0), (0, 0), (1, 0), (0, 0), (0, 0)))
                return jnp.concatenate([p[:, :, :nw], p[:, :, 1:]], axis=3)
            bk2, bv2 = (look(bk), look(bv))
            seq = jnp.arange(n).reshape(nw, w)
            seq_p = jnp.pad(seq, ((1, 0), (0, 0)), constant_values=-1)
            jt = jnp.concatenate([seq_p[:nw], seq_p[1:]], axis=1)
            it = seq[:, :, None]
            jb = jt[:, None, :]
            mask = (it < jb) | (it > jb + w) | (jb == -1)
            sim = jnp.einsum('bhwie,bhwje->bhwij', bq, bk2) * QK_SCALE
            sim = jnp.where(mask, -jnp.finfo(sim.dtype).max, sim)
            attn = jax.nn.softmax(sim, -1)
            out = jnp.einsum('bhwij,bhwje->bhwie', attn, bv2)
            return out.reshape(b, h, n, d)

        def attn_layer(x, Wqkv, qs, ksc, Wo):
            b, n, _ = x.shape
            qkv = x @ Wqkv
            q, k, v = jnp.split(qkv, 3, -1)
            sh = lambda t: t.reshape(b, n, HEADS, DIM_HEAD).transpose(0, 2, 1, 3)
            q, k, v = (sh(q), sh(k), sh(v))
            q = l2norm(q) * qs
            k = l2norm(k) * ksc
            freqs, scale = rotary_tables(n)
            cos, sin = (jnp.cos(freqs), jnp.sin(freqs))
            q = q * cos * scale + rotate_half(q) * sin * scale
            inv = 1.0 / scale
            k = k * cos * inv + rotate_half(k) * sin * inv
            out = local_attention(q, k, v)
            out = out.transpose(0, 2, 1, 3).reshape(b, n, INNER)
            return out @ Wo

        def ffn_layer(x, g, bln, W1, b1, W2, b2):
            mu = x.mean(-1, keepdims=True)
            var = ((x - mu) ** 2).mean(-1, keepdims=True)
            xn = (x - mu) / jnp.sqrt(var + 1e-05) * g + bln
            hg = xn @ W1 + b1
            a, gate = jnp.split(hg, 2, -1)
            return a * jax.nn.gelu(gate, approximate=False) @ W2 + b2
        key = jax.random.key(seed)
        ks = jax.random.split(key, 8)
        B, N = (2, 256)
        init = lambda k, shape: jax.random.normal(k, shape, jnp.float32) * 0.02
        return {'x': jax.random.normal(ks[0], (B, N, DIM), jnp.float32), 'Wqkv': init(ks[1], (DEPTH, DIM, 3 * INNER)), 'q_scale': jnp.ones((DEPTH, DIM_HEAD), jnp.float32), 'k_scale': jnp.ones((DEPTH, DIM_HEAD), jnp.float32), 'Wo': init(ks[2], (DEPTH, INNER, DIM)), 'ln_g': jnp.ones((DEPTH, DIM), jnp.float32), 'ln_b': jnp.zeros((DEPTH, DIM), jnp.float32), 'W1': init(ks[3], (DEPTH, DIM, 2 * DIM_INNER)), 'b1': jnp.zeros((DEPTH, 2 * DIM_INNER), jnp.float32), 'W2': init(ks[4], (DEPTH, DIM_INNER, DIM)), 'b2': jnp.zeros((DEPTH, DIM), jnp.float32)}
    _L0_ffn_in = _L0_ffn_setup()
    _d = {'L0_attn_x': _L0_attn_in['x'], 'L0_attn_Wq': _L0_attn_in['Wq'], 'L0_attn_Wk': _L0_attn_in['Wk'], 'L0_attn_Wv': _L0_attn_in['Wv'], 'L0_attn_Wo': _L0_attn_in['Wo'], 'L0_ffn_Wqkv': _L0_ffn_in['Wqkv'], 'L0_ffn_q_scale': _L0_ffn_in['q_scale'], 'L0_ffn_k_scale': _L0_ffn_in['k_scale'], 'L0_ffn_Wo': _L0_ffn_in['Wo'], 'L0_ffn_ln_g': _L0_ffn_in['ln_g'], 'L0_ffn_ln_b': _L0_ffn_in['ln_b'], 'L0_ffn_W1': _L0_ffn_in['W1'], 'L0_ffn_b1': _L0_ffn_in['b1'], 'L0_ffn_W2': _L0_ffn_in['W2'], 'L0_ffn_b2': _L0_ffn_in['b2']}
    _x0 = _d['L0_attn_x']
    _d['L0_attn_x'] = jax.random.normal(jax.random.fold_in(jax.random.key(seed), 1), (2, 1024, 128), dtype=_x0.dtype)
    del _x0
    return _d

def reference(L0_attn_x, L0_attn_Wq, L0_attn_Wk, L0_attn_Wv, L0_attn_Wo, L0_ffn_Wqkv, L0_ffn_q_scale, L0_ffn_k_scale, L0_ffn_Wo, L0_ffn_ln_g, L0_ffn_ln_b, L0_ffn_W1, L0_ffn_b1, L0_ffn_W2, L0_ffn_b2):

    def _L0_attn_ref(x, Wq, Wk, Wv, Wo):
        import jax, jax.numpy as jnp
        import numpy as np
        D_MODEL = 128
        N_HEADS = 16
        D_HEAD = D_MODEL // N_HEADS
        WINDOW = 32
        CAUSAL = True
        NEG = -1000000000.0

        def build_sliding_window_mask(seq_len, window_size, causal=True):
            i = jnp.arange(seq_len)[:, None]
            j = jnp.arange(seq_len)[None, :]
            if causal:
                attend = (j <= i) & (j >= i - window_size)
            else:
                half = window_size // 2
                attend = jnp.abs(j - i) <= half
            return jnp.where(attend, 0.0, NEG).astype(jnp.float32)
        B, T, _ = x.shape

        def split_heads(y):
            return y.reshape(B, T, N_HEADS, D_HEAD).transpose(0, 2, 1, 3)
        Q = split_heads(x @ Wq.T)
        K = split_heads(x @ Wk.T)
        V = split_heads(x @ Wv.T)
        scale = 1.0 / np.sqrt(D_HEAD)
        mask = build_sliding_window_mask(T, WINDOW, causal=CAUSAL)
        scores = jnp.einsum('bhqd,bhkd->bhqk', Q, K) * scale + mask
        weights = jax.nn.softmax(scores, axis=-1)
        out = jnp.einsum('bhqk,bhkd->bhqd', weights, V)
        out = out.transpose(0, 2, 1, 3).reshape(B, T, D_MODEL)
        return out @ Wo.T

    def _L0_ffn_ref(x, Wqkv, q_scale, k_scale, Wo, ln_g, ln_b, W1, b1, W2, b2):
        import jax, jax.numpy as jnp
        import numpy as np
        DIM = 128
        DEPTH = 6
        HEADS = 16
        DIM_HEAD = 64
        WINDOW = 32
        INNER = HEADS * DIM_HEAD
        DIM_INNER = int(DIM * 4 * 2 / 3)
        QK_SCALE = 8.0

        def shift_tokens(t):
            a, s = jnp.split(t, 2, -1)
            s = jnp.pad(s, ((0, 0), (1, 0), (0, 0)))[:, :-1]
            return jnp.concatenate([a, s], -1)

        def l2norm(t):
            return t / jnp.maximum(jnp.linalg.norm(t, axis=-1, keepdims=True), 1e-12)

        def rotate_half(x):
            x1, x2 = jnp.split(x, 2, -1)
            return jnp.concatenate([-x2, x1], -1)

        def rotary_tables(n):
            half = jnp.arange(0, DIM_HEAD, 2, dtype=jnp.float32)
            inv_freq = 1.0 / 10000.0 ** (half / DIM_HEAD)
            t = jnp.arange(n, dtype=jnp.float32)
            freqs = t[:, None] * inv_freq[None, :]
            freqs = jnp.concatenate([freqs, freqs], -1)
            base_scale = (half + 0.4 * DIM_HEAD) / (1.4 * DIM_HEAD)
            power = (t - n // 2) / (WINDOW // 2)
            scale = base_scale[None, :] ** power[:, None]
            scale = jnp.concatenate([scale, scale], -1)
            return (freqs, scale)

        def local_attention(q, k, v):
            b, h, n, d = q.shape
            w = WINDOW
            nw = n // w
            bq = q.reshape(b, h, nw, w, d)
            bk = k.reshape(b, h, nw, w, d)
            bv = v.reshape(b, h, nw, w, d)

            def look(t):
                p = jnp.pad(t, ((0, 0), (0, 0), (1, 0), (0, 0), (0, 0)))
                return jnp.concatenate([p[:, :, :nw], p[:, :, 1:]], axis=3)
            bk2, bv2 = (look(bk), look(bv))
            seq = jnp.arange(n).reshape(nw, w)
            seq_p = jnp.pad(seq, ((1, 0), (0, 0)), constant_values=-1)
            jt = jnp.concatenate([seq_p[:nw], seq_p[1:]], axis=1)
            it = seq[:, :, None]
            jb = jt[:, None, :]
            mask = (it < jb) | (it > jb + w) | (jb == -1)
            sim = jnp.einsum('bhwie,bhwje->bhwij', bq, bk2) * QK_SCALE
            sim = jnp.where(mask, -jnp.finfo(sim.dtype).max, sim)
            attn = jax.nn.softmax(sim, -1)
            out = jnp.einsum('bhwij,bhwje->bhwie', attn, bv2)
            return out.reshape(b, h, n, d)

        def attn_layer(x, Wqkv, qs, ksc, Wo):
            b, n, _ = x.shape
            qkv = x @ Wqkv
            q, k, v = jnp.split(qkv, 3, -1)
            sh = lambda t: t.reshape(b, n, HEADS, DIM_HEAD).transpose(0, 2, 1, 3)
            q, k, v = (sh(q), sh(k), sh(v))
            q = l2norm(q) * qs
            k = l2norm(k) * ksc
            freqs, scale = rotary_tables(n)
            cos, sin = (jnp.cos(freqs), jnp.sin(freqs))
            q = q * cos * scale + rotate_half(q) * sin * scale
            inv = 1.0 / scale
            k = k * cos * inv + rotate_half(k) * sin * inv
            out = local_attention(q, k, v)
            out = out.transpose(0, 2, 1, 3).reshape(b, n, INNER)
            return out @ Wo

        def ffn_layer(x, g, bln, W1, b1, W2, b2):
            mu = x.mean(-1, keepdims=True)
            var = ((x - mu) ** 2).mean(-1, keepdims=True)
            xn = (x - mu) / jnp.sqrt(var + 1e-05) * g + bln
            hg = xn @ W1 + b1
            a, gate = jnp.split(hg, 2, -1)
            return a * jax.nn.gelu(gate, approximate=False) @ W2 + b2
        for i in range(DEPTH):
            x = attn_layer(shift_tokens(x), Wqkv[i], q_scale[i], k_scale[i], Wo[i]) + x
            x = ffn_layer(shift_tokens(x), ln_g[i], ln_b[i], W1[i], b1[i], W2[i], b2[i]) + x
        return x
    x = L0_attn_x
    x = x + 0.5 * _L0_ffn_ref(_layernorm(x, axis=-1), L0_ffn_Wqkv, L0_ffn_q_scale, L0_ffn_k_scale, L0_ffn_Wo, L0_ffn_ln_g, L0_ffn_ln_b, L0_ffn_W1, L0_ffn_b1, L0_ffn_W2, L0_ffn_b2)
    x = x + _L0_attn_ref(_layernorm(x, axis=-1), L0_attn_Wq, L0_attn_Wk, L0_attn_Wv, L0_attn_Wo)
    x = x + 0.5 * _L0_ffn_ref(_layernorm(x, axis=-1), L0_ffn_Wqkv, L0_ffn_q_scale, L0_ffn_k_scale, L0_ffn_Wo, L0_ffn_ln_g, L0_ffn_ln_b, L0_ffn_W1, L0_ffn_b1, L0_ffn_W2, L0_ffn_b2)
    return x

_drawn_inputs = setup_inputs


def setup_inputs(seed=0):
    import zlib

    import numpy as np

    out = dict(_drawn_inputs(seed))
    spreads = {'L0_ffn_q_scale': (1.0, 0.6),
     'L0_ffn_k_scale': (1.0, 0.6),
     'L0_ffn_ln_g': (1.0, 0.6),
     'L0_ffn_ln_b': (0.0, 0.8),
     'L0_ffn_b1': (0.0, 0.8),
     'L0_ffn_b2': (0.0, 0.1)}
    factors = {'L0_ffn_W1': 3.17, 'L0_ffn_W2': 3.097}
    for name, (base, spread) in spreads.items():
        noise = np.random.default_rng([zlib.crc32(name.encode()), seed]).standard_normal(out[name].shape)
        drawn = base * np.exp(spread * noise) if base else spread * noise
        out[name] = jnp.asarray(drawn.astype(out[name].dtype))
    for name, factor in factors.items():
        out[name] = (out[name] * factor).astype(out[name].dtype)
    return out
```

```python
from contextlib import ExitStack

import numpy as np

import concourse.bass as bass
from concourse import mybir

FP32 = mybir.dt.float32
BF16 = mybir.dt.bfloat16
INT32 = mybir.dt.int32
ALU = mybir.AluOpType
ACT = mybir.ActivationFunctionType
AX_X = mybir.AxisListType.X

P = 128
BATCH, SEQ, DIM = 2, 1024, 128
DEPTH, HEADS, DHEAD = 6, 16, 64
WINDOW = 32
INNER = HEADS * DHEAD
FF = int(DIM * 4 * 2 / 3)
FFB = [P, P, FF - 2 * P]
TILES = BATCH * SEQ // P
PAIRS = TILES // 2
TPB = SEQ // P
PADDED = WINDOW + SEQ
KEYS = 64 + WINDOW
QUAD = 4 * KEYS
BODIES = DEPTH * PAIRS
MASKED = -1.0e30
RSQRT_MAGIC = float(0x5F3759DF)
STEPS = 11
CHUNKS = ["v0", "v1", "q0", "k0", "q1", "k1"]
TURN_A = ["QT0", "KT0", "QT1", "KT1", "*XT", "PT0", "PT1", "OT0", "PT2", "PT3", "OT1"]
TURN_B = ["QT0", "KT0", "QT1", "KT1", "*XN", "*H0", "*H1", "*H2", "PT0", "PT1", "OT0", "PT2", "PT3",
          "OT1", "*FO", "WO"]
TURN = ["A" + x for x in TURN_A] + ["B" + x for x in TURN_B]
FIRST_TURN = [x for x in TURN if "*" not in x]
SKIPPED = len(TURN) - len(FIRST_TURN)


def job(n, name):
    if isinstance(n, int) and n == 0:
        return FIRST_TURN.index(name)
    if isinstance(n, int) and n == BODIES:
        return len(TURN) * BODIES - SKIPPED + ["A*XT", "B*XN", "B*H0", "B*H1", "B*H2", "B*FO"].index(name)
    return n * len(TURN) + (TURN.index(name) - SKIPPED)


def bank_of(n, name):
    if isinstance(n, int):
        return 5 + job(n, name) % 3
    return 5 + (TURN.index(name) - SKIPPED) % 3


assert len(TURN) % 3 == 0 and SKIPPED % 3 == 0


def wait(eng, sem, value):
    if not (isinstance(value, int) and value <= 0):
        eng.wait_ge(sem, value)


def known(eng, value):
    return value if isinstance(value, int) else eng.snap(value)


def pair_column(n):
    p = n % PAIRS
    return p * (2 * P) + p // (PAIRS // 2) * WINDOW + WINDOW


def over_turns(eng, body):
    body(0)
    with eng.Fori(1, BODIES - 1) as n:
        body(n)
    body(BODIES - 1)


def heads4(ap):
    return ap.rearrange("p (h k) -> p h k", h=4)


def spread(ap, shape):
    return ap.unsqueeze(2).broadcast_to(shape)


class Rsqrt:

    def __init__(self, eng, done, count, x, xc, y, a, b):
        self.eng, self.done, self.count = eng, done, count
        self.x, self.xc, self.y, self.a, self.b = x, xc, y, a, b
        self.k = 0

    def step(self):
        e, k = self.eng, self.k
        if k:
            e.wait_ge(self.done, self.count + k)
        if k == 0:
            i = e.tensor_scalar(self.xc, self.x, 1e-24, None, ALU.max)
        elif k == 1:
            i = e.tensor_scalar(self.y.bitcast(INT32), self.xc.bitcast(INT32), -0.5, RSQRT_MAGIC, ALU.mult, ALU.add)
        elif k % 3 == 2:
            i = e.scalar_tensor_tensor(self.a, self.y, -0.5, self.y, ALU.mult, ALU.mult)
        elif k % 3 == 0:
            i = e.tensor_tensor(self.b, self.a, self.xc, ALU.mult)
        else:
            i = e.scalar_tensor_tensor(self.y, self.b, 1.5, self.y, ALU.add, ALU.mult)
        i.then_inc(self.done, 1)
        self.k += 1

    def rest(self):
        while self.k < STEPS:
            self.step()


def layernorm_to_columns(nc, base, xT, ident, psum, name):
    with ExitStack() as ctx:
        sb = lambda n, s: ctx.enter_context(nc.sbuf_tensor(f"{name}_{n}", s, FP32))
        sem = lambda n: ctx.enter_context(nc.semaphore(f"{name}_{n}"))
        centred, square = sb("centred", [P, TILES, DIM]), sb("square", [P, TILES, DIM])
        mean, var, varc = sb("mean", [P, TILES]), sb("var", [P, TILES]), sb("varc", [P, TILES])
        rstd, ta, tb = sb("rstd", [P, TILES]), sb("ta", [P, TILES]), sb("tb", [P, TILES])
        stats, newton, normed, turned, evacuated = (sem(x) for x in ("stats", "newton", "normed", "turned", "evacuated"))
        block = ctx.enter_context(nc.Block())

        @block.vector
        def _(dve):
            full = [P, TILES, DIM]
            dve.tensor_reduce(mean[:], base[:], AX_X, ALU.add).then_inc(stats, 1)
            dve.wait_ge(stats, 1)
            dve.tensor_scalar(mean[:], mean[:], -1.0 / DIM, None, ALU.mult).then_inc(stats, 1)
            dve.wait_ge(stats, 2)
            dve.tensor_tensor(centred[:], base[:], spread(mean[:], full), ALU.add).then_inc(stats, 1)
            dve.wait_ge(stats, 3)
            dve.tensor_tensor(square[:], centred[:], centred[:], ALU.mult).then_inc(stats, 1)
            dve.wait_ge(stats, 4)
            dve.tensor_reduce(var[:], square[:], AX_X, ALU.add).then_inc(stats, 1)
            dve.wait_ge(stats, 5)
            dve.tensor_scalar(var[:], var[:], 1.0 / DIM, 1e-5, ALU.mult, ALU.add).then_inc(stats, 1)
            dve.wait_ge(stats, 6)
            Rsqrt(dve, newton, 0, var[:], varc[:], rstd[:], ta[:], tb[:]).rest()
            dve.wait_ge(newton, STEPS)
            dve.tensor_tensor(centred[:], centred[:], spread(rstd[:], full), ALU.mult).then_inc(normed, 1)

        @block.tensor
        def _(pe):
            pe.wait_ge(normed, 1)
            for t in range(TILES):
                last = nc.tensor.transpose(psum[:, t // 4, t % 4 * P:(t % 4 + 1) * P], centred[:, t, :], ident[:])
                if t % 4 == 3:
                    last.then_inc(turned, 1)

        @block.scalar
        def _(act):
            for g in range(TILES // 4):
                act.wait_ge(turned, g + 1)
                c = pair_column(2 * g)
                nc.scalar.activation(xT[:, c:c + 4 * P], psum[:, g, :], ACT.Copy).then_inc(evacuated, 1)


def add_half_of_columns(nc, base, xT, ident, psum, name):
    with ExitStack() as ctx:
        sem = lambda n: ctx.enter_context(nc.semaphore(f"{name}_{n}"))
        turned, added = sem("turned"), sem("added")
        block = ctx.enter_context(nc.Block())

        @block.tensor
        def _(pe):
            for t in range(TILES):
                c = pair_column(t // 2) + t % 2 * P
                last = nc.tensor.transpose(psum[:, t // 4, t % 4 * P:(t % 4 + 1) * P], xT[:, c:c + P], ident[:])
                if t % 4 == 3:
                    last.then_inc(turned, 1)

        @block.vector
        def _(dve):
            for g in range(TILES // 4):
                dve.wait_ge(turned, g + 1)
                tiles = base[:, 4 * g:4 * g + 4, :].rearrange("p t d -> p (t d)")
                dve.scalar_tensor_tensor(tiles, psum[:, g, :], 0.5, tiles, ALU.mult, ALU.add).then_inc(added, 1)


def stack(nc, dram, const, xT, psum, name):
    ident, ident16, masks, tables = const["ident"], const["ident16"], const["masks"], const["tables"]
    inside = const["inside"]
    ctx = ExitStack()
    with ctx:
        def sb(n, shape, dt=FP32):
            return ctx.enter_context(nc.sbuf_tensor(f"{name}_{n}", shape, dt))

        def sem(n):
            return ctx.enter_context(nc.semaphore(f"{name}_{n}"))

        w_qkv = sb("w_qkv", [P, 3 * INNER])
        w_o = sb("w_o", [P, INNER // P, DIM])
        w_1 = sb("w_1", [P, 2 * FF])
        w_2 = sb("w_2", [P, 3, DIM])
        ffn_cols = sb("ffn_cols", [P, 9])
        qk_scales = sb("qk_scales", [P, 4 * DHEAD])
        x1T = sb("x1T", [P, BATCH * PADDED])
        xs = sb("xs", [P, 2, P])
        turn_tables = sb("turn_tables", [P, 2, 4 * DHEAD])
        squares = sb("squares", [P, 4, 512])
        norm2 = sb("norm2", [P, 2 * HEADS + 2])
        norm2c = sb("norm2c", [P, 2 * HEADS + 2])
        rnorm = sb("rnorm", [P, 2 * HEADS + 2])
        na, nb = sb("na", [P, 2 * HEADS + 2]), sb("nb", [P, 2 * HEADS + 2])
        straight = sb("straight", [P, 4, 512])
        crossed = sb("crossed", [P, 4, 512])
        qk = sb("qk", [P, 4, 512])
        qT = sb("qT", [P, 8, P])
        kT = sb("kT", [P, 2, 8, 2, WINDOW + P])
        v_tok = sb("v_tok", [P, 2, INNER])
        v_win = sb("v_win", [KEYS, 2, 2, INNER])
        top = sb("top", [P, HEADS])
        shifted = sb("shifted", [P, 4, QUAD])
        probs = sb("probs", [P, 4, QUAD])
        total, rtotal = sb("total", [P, HEADS]), sb("rtotal", [P, HEADS])
        probs_n = sb("probs_n", [P, 4, QUAD])
        pT = sb("pT", [KEYS, 4, 4 * P])
        oT = sb("oT", [P, 8, 2 * P])
        y1 = sb("y1", [P, 2 * P])
        xs2 = sb("xs2", [P, 2 * P])
        x_tok = sb("x_tok", [P, 2, P])
        lmean = sb("lmean", [P, 2])
        xc_tok = sb("xc_tok", [P, 2, P])
        lsq = sb("lsq", [P, 2, P])
        xn_tok = sb("xn_tok", [P, 2, P])
        xnT = sb("xnT", [P, 2 * P])
        up = sb("up", [P, 3, 2 * P])
        gate = sb("gate", [P, 3, 2 * P])
        hidden = sb("hidden", [P, 3, 2 * P])
        y2 = sb("y2", [P, 2 * P])

        proj_full, s_full, tr_full = sem("proj_full"), sem("s_full"), sem("tr_full")
        tr_evac, v_evac, squared, exp_done = sem("tr_evac"), sem("v_evac"), sem("squared"), sem("exp_done")
        zeroed = sem("zeroed")
        xs_done, max_done, s_sub, sum_done, rec_done = (sem(x) for x in ("xs_done", "max_done", "s_sub", "sum_done", "rec_done"))
        rotary_done, norm2_done, newton = sem("rotary_done"), sem("norm2_done"), sem("newton")
        kprev_done, x1_done, xs2_done, ln_done, xn_done = (sem(x) for x in ("kprev_done", "x1_done", "xs2_done", "ln_done", "xn_done"))
        hidden_done, x2_done = sem("hidden_done"), sem("x2_done")
        tables_done, probs_normed, qk_added, qk_normed = (sem(x) for x in ("tables_done", "probs_normed", "qk_added", "qk_normed"))
        qkv_loaded, scales_loaded, wo_loaded, ffn_loaded, v_moved = (sem(x) for x in ("qkv_loaded", "scales_loaded", "wo_loaded", "ffn_loaded", "v_moved"))

        block = ctx.enter_context(nc.Block())

        def s_bank(q):
            return psum[:, 3 + q % 2, 0:QUAD]

        @block.sync
        def _(sp):
            def load_qkv(l):
                folded, l = known(sp, TILES * l), known(sp, l)
                wait(sp, proj_full, known(sp, 6 * TILES * l))
                sp.dma_start(w_qkv[:], dram["Wqkv"][bass.ds(l, 1), :, :].rearrange("o p n -> p (o n)")).then_inc(qkv_loaded, 16)
                wait(sp, tables_done, folded)
                sp.dma_start(qk_scales[:], dram["qk_scales"][bass.ds(l, 1), :, :].rearrange("o p n -> p (o n)")).then_inc(scales_loaded, 16)

            def load_wo(l):
                if not (isinstance(l, int) and l == 0):
                    wait(sp, tr_full, known(sp, job(PAIRS * l - 1, "BWO") + 1))
                sp.dma_start(w_o[:], dram["Wo"][bass.ds(l, 1), :, :].rearrange("o (j p) n -> p (o j) n", p=P)).then_inc(wo_loaded, 16)

            def load_ffn(l):
                wait(sp, x2_done, known(sp, PAIRS * l))
                sp.dma_start(w_1[:], dram["W1"][bass.ds(l, 1), :, :].rearrange("o p n -> p (o n)")).then_inc(ffn_loaded, 16)
                sp.dma_start(w_2[:, 0:2, :], dram["W2"][bass.ds(l, 1), 0:2 * P, :].rearrange("o (j p) n -> p (o j) n", p=P)).then_inc(ffn_loaded, 16)
                sp.dma_start(w_2[0:FFB[2], 2, :], dram["W2"][bass.ds(l, 1), 2 * P:FF, :].rearrange("o p n -> p (o n)")).then_inc(ffn_loaded, 16)
                sp.dma_start(ffn_cols[:], dram["ffn_cols"][bass.ds(l, 1), :, :].rearrange("o p n -> p (o n)")).then_inc(ffn_loaded, 16)

            def move_v(n, s):
                wait(sp, v_evac, 2 * (2 * n + s) + 2)
                now, before = v_tok[:, s, :], v_tok[:, 1 - s, :]
                sp.dma_start(v_win[0:WINDOW, s, 0, :], before[P - WINDOW:P, :]).then_inc(v_moved, 16)
                sp.dma_start(v_win[WINDOW:KEYS, s, 0, :], now[0:64, :]).then_inc(v_moved, 16)
                sp.dma_start(v_win[:, s, 1, :], now[WINDOW:P, :]).then_inc(v_moved, 16)

            def layer(l, first, last):
                n = PAIRS * l
                move_v(n, 1)
                if not first:
                    load_wo(l)
                move_v(n + 1, 0)
                if not first:
                    load_ffn(l)
                move_v(n + 1, 1)
                move_v(n + 2, 0)
                with sp.Fori(2, PAIRS - 1) as p:
                    move_v(n + p, 1)
                    move_v(n + p + 1, 0)
                move_v(n + PAIRS - 1, 1)
                if not last:
                    load_qkv(l + 1)
                    move_v(n + PAIRS, 0)

            load_qkv(0)
            load_wo(0)
            load_ffn(0)
            sp.wait_ge(zeroed, 2)
            move_v(0, 0)
            layer(0, True, False)
            with sp.Fori(1, DEPTH - 1) as l:
                layer(l, False, False)
            layer(DEPTH - 1, False, True)

        @block.tensor
        def _(pe):
            def project(i, c):
                if c == 0:
                    pe.wait_ge(xs_done, i + 1)
                at = {"v": 2 * INNER, "q": 0, "k": INNER}[CHUNKS[c][0]] + 512 * int(CHUNKS[c][1])
                if c < 3:
                    wait(pe, norm2_done, 4 * (i - 1) + 2 + c)
                elif c < 5:
                    wait(pe, v_evac, 2 * i + c - 2)
                else:
                    wait(pe, norm2_done, 4 * i + 1)
                par = 0 if isinstance(i, int) and i == 0 else project.parity
                nc.tensor.matmul(psum[:, c % 3, :], xs[:, par, :], w_qkv[:, at:at + 512],
                                 start=True, stop=True).then_inc(proj_full, 1)

            def scores(n, s, q):
                i = 2 * n + s
                wait(pe, s_sub, 4 * i + q - 1)
                if q == 0:
                    pe.wait_ge(tr_evac, job(n, "AB"[s] + "KT0") + 1)
                    wait(pe, kprev_done, i)
                if q == 2:
                    pe.wait_ge(tr_evac, job(n, "AB"[s] + "KT1") + 1)
                mask = masks[:, bass.ds(n % (TPB // 2) * QUAD, QUAD)] if s == 0 else masks[:, QUAD:2 * QUAD]
                nc.tensor.matmul(s_bank(q), ident16[:], mask, start=True, stop=False, skip_group_check=True)
                for pr in range(2):
                    for b in range(2):
                        last = nc.tensor.matmul(
                            s_bank(q)[64 * b:64 * b + 64, pr * 2 * KEYS:(pr + 1) * 2 * KEYS],
                            qT[:, 2 * q + pr, 64 * b:64 * b + 64], kT[:, s, 2 * q + pr, :, 64 * b:64 * b + KEYS],
                            start=False, stop=True, skip_group_check=True)
                last.then_inc(s_full, 1)

            def tenant(n, name):
                wait(pe, tr_evac, job(n, name) - 2)
                return psum[:, bank_of(n, name), :]

            def turn_qk(n, s, what, half):
                name = "AB"[s] + what + str(half)
                bank = tenant(n, name)
                c = CHUNKS.index(what[0].lower() + str(half)) - 2
                pe.wait_ge(qk_normed, 4 * (2 * n + s) + c + 1)
                for j in range(4):
                    last = nc.tensor.transpose(bank[:, j * P:(j + 1) * P], qk[:, c, j * P:(j + 1) * P], ident[:])
                last.then_inc(tr_full, 1)

            def turn_probs(n, s, q):
                bank = tenant(n, "AB"[s] + f"PT{q}")
                pe.wait_ge(probs_normed, 4 * (2 * n + s) + q + 1)
                for h in range(4):
                    last = nc.tensor.transpose(bank[0:KEYS, h * P:(h + 1) * P], probs_n[:, q, h * KEYS:(h + 1) * KEYS], ident[:])
                last.then_inc(tr_full, 1)

            def times_v(n, s, half):
                name = "AB"[s] + f"OT{half}"
                bank = tenant(n, name)
                pe.wait_ge(tr_evac, job(n, "AB"[s] + f"PT{2 * half + 1}") + 1)
                if half == 0:
                    pe.wait_ge(v_moved, 48 * (2 * n + s) + 48)
                for pr in range(4):
                    for b in range(2):
                        for h2 in range(2):
                            h = 8 * half + 2 * pr + h2
                            last = nc.tensor.matmul(
                                bank[64 * h2:64 * h2 + 64, pr * P + 64 * b:pr * P + 64 * b + 64],
                                v_win[:, s, b, h * DHEAD:(h + 1) * DHEAD],
                                pT[:, h // 4, h % 4 * P + 64 * b:h % 4 * P + 64 * b + 64],
                                start=True, stop=True, skip_group_check=True)
                last.then_inc(tr_full, 1)

            def times_wo(n):
                bank = tenant(n, "BWO")
                pe.wait_ge(tr_evac, job(n, "BOT1") + 1)
                pe.wait_ge(wo_loaded, n // PAIRS * 16 + 16)
                for j in range(8):
                    last = nc.tensor.matmul(bank[:, 0:2 * P], w_o[:, j, :], oT[:, j, :], start=(j == 0), stop=(j == 7))
                last.then_inc(tr_full, 1)

            def ffn_tokens(n):
                bank = tenant(n, "A*XT")
                pe.wait_ge(xs2_done, n)
                for t in range(2):
                    last = nc.tensor.transpose(bank[:, t * P:(t + 1) * P], xs2[:, t * P:(t + 1) * P], ident[:])
                last.then_inc(tr_full, 1)

            def ffn_columns(n):
                bank = tenant(n, "B*XN")
                pe.wait_ge(xn_done, n)
                for t in range(2):
                    last = nc.tensor.transpose(bank[:, t * P:(t + 1) * P], xn_tok[:, t, :], ident[:])
                last.then_inc(tr_full, 1)

            def ffn_up(n, j):
                bank = tenant(n, f"B*H{j}")
                if j == 0:
                    pe.wait_ge(tr_evac, job(n, "B*XN") + 1)
                    pe.wait_ge(ffn_loaded, (n - 1) // PAIRS * 64 + 64)
                m = FFB[j]
                nc.tensor.matmul(bank[0:m, 0:2 * P], w_1[:, j * P:j * P + m], xnT[:], start=True, stop=True, skip_group_check=True)
                nc.tensor.matmul(bank[0:m, 2 * P:4 * P], w_1[:, FF + j * P:FF + j * P + m], xnT[:],
                                 start=True, stop=True, skip_group_check=True).then_inc(tr_full, 1)

            def ffn_down(n):
                bank = tenant(n, "B*FO")
                pe.wait_ge(hidden_done, 3 * n)
                for j, m in enumerate(FFB):
                    last = nc.tensor.matmul(bank[:, 0:2 * P], w_2[0:m, j, :], hidden[0:m, j, :], start=(j == 0), stop=(j == 2))
                last.then_inc(tr_full, 1)

            def turn(n):
                first = isinstance(n, int) and n == 0
                last = isinstance(n, int) and n == BODIES - 1
                for s in range(2):
                    more = not (last and s == 1)
                    i1 = 2 * n + s + 1
                    project.parity = 1 - s
                    for half in range(2):
                        turn_qk(n, s, "QT", half)
                        turn_qk(n, s, "KT", half)
                    if not first:
                        (ffn_columns if s else ffn_tokens)(n)
                    scores(n, s, 0)
                    scores(n, s, 1)
                    if more:
                        if s == 1:
                            pe.wait_ge(qkv_loaded, (n + 1) // PAIRS * 16 + 16)
                        project(i1, 0)
                        project(i1, 1)
                    scores(n, s, 2)
                    if more:
                        project(i1, 2)
                    scores(n, s, 3)
                    if more:
                        project(i1, 3)
                    if s and not first:
                        ffn_up(n, 0)
                    if more:
                        project(i1, 4)
                    if s and not first:
                        ffn_up(n, 1)
                    if more:
                        project(i1, 5)
                    if s and not first:
                        ffn_up(n, 2)
                    for half in range(2):
                        turn_probs(n, s, 2 * half)
                        turn_probs(n, s, 2 * half + 1)
                        times_v(n, s, half)
                    if s:
                        if not first:
                            ffn_down(n)
                        times_wo(n)

            pe.wait_ge(qkv_loaded, 16)
            for c in range(6):
                project(0, c)
            over_turns(pe, turn)
            ffn_tokens(BODIES)
            ffn_columns(BODIES)
            for j in range(3):
                ffn_up(BODIES, j)
            ffn_down(BODIES)

        @block.scalar
        def _(act):
            def evac(n, name):
                act.wait_ge(tr_full, job(n, name) + 1)
                return psum[:, bank_of(n, name), :]

            def evac_q(n, s, half):
                bank = evac(n, "AB"[s] + f"QT{half}")
                wait(act, s_full, 4 * (2 * n + s))
                nc.scalar.activation(qT[:, 4 * half:4 * half + 4, :], bank.rearrange("p (j t) -> p j t", j=4),
                                     ACT.Copy).then_inc(tr_evac, 1)

            def evac_k(n, s, half):
                bank = evac(n, "AB"[s] + f"KT{half}").rearrange("p (j t) -> p j t", j=4)
                act.wait_ge(zeroed, 2)
                for h2 in range(2):
                    r = slice(64 * h2, 64 * h2 + 64)
                    last = nc.scalar.activation(kT[r, s, 4 * half:4 * half + 4, h2, WINDOW:], bank[r], ACT.Copy)
                last.then_inc(tr_evac, 1)

            def evac_v(i, par, c):
                act.wait_ge(proj_full, 6 * i + c + 1)
                wait(act, v_moved, 48 * i)
                nc.scalar.activation(v_tok[:, par, 512 * c:512 * c + 512], psum[:, c, :], ACT.Copy).then_inc(v_evac, 1)

            def square(i, c):
                act.wait_ge(proj_full, 6 * i + c + 3)
                wait(act, norm2_done, 4 * (i - 1) + c + 1)
                nc.scalar.activation(squares[:, c, :], psum[:, (c + 2) % 3, :], ACT.Square).then_inc(squared, 1)

            def exps(n, s, q):
                i = 2 * n + s
                act.wait_ge(s_sub, 4 * i + q + 1)
                wait(act, probs_normed, 4 * (i - 1) + q + 1)
                nc.scalar.activation(probs[:, q, :], shifted[:, q, :], ACT.Exp, scale=8.0).then_inc(exp_done, 1)

            def evac_p(n, s, q):
                bank = evac(n, "AB"[s] + f"PT{q}")
                nc.scalar.activation(pT[:, q, :], bank[0:KEYS, :], ACT.Copy).then_inc(tr_evac, 1)

            def evac_o(n, s, half):
                bank = evac(n, "AB"[s] + f"OT{half}")
                nc.scalar.activation(oT[:, 4 * half:4 * half + 4, s * P:(s + 1) * P], bank.rearrange("p (j t) -> p j t", j=4),
                                     ACT.Copy).then_inc(tr_evac, 1)

            def evac_wo(n):
                bank = evac(n, "BWO")
                wait(act, x1_done, n)
                nc.scalar.activation(y1[:], bank[:, 0:2 * P], ACT.Copy).then_inc(tr_evac, 1)

            def evac_ffn_tokens(n):
                bank = evac(n, "A*XT")
                nc.scalar.activation(x_tok[:], bank[:, 0:2 * P].rearrange("p (t d) -> p t d", t=2), ACT.Copy).then_inc(tr_evac, 1)

            def evac_ffn_columns(n):
                bank = evac(n, "B*XN")
                act.wait_ge(ffn_loaded, (n - 1) // PAIRS * 64 + 64)
                nc.scalar.activation(xnT[:], bank[:, 0:2 * P], ACT.Identity, bias=ffn_cols[:, 1:2], scale=ffn_cols[:, 0:1]).then_inc(tr_evac, 1)

            def evac_up(n, j):
                m = FFB[j]
                bank = evac(n, f"B*H{j}")
                wait(act, hidden_done, 3 * (n - 1))
                nc.scalar.activation(gate[0:m, j, :], bank[0:m, 2 * P:4 * P], ACT.Gelu, bias=ffn_cols[0:m, 5 + j:6 + j])
                nc.scalar.activation(up[0:m, j, :], bank[0:m, 0:2 * P], ACT.Identity, bias=ffn_cols[0:m, 2 + j:3 + j]).then_inc(tr_evac, 1)

            def evac_down(n):
                bank = evac(n, "B*FO")
                wait(act, x2_done, n - 1)
                nc.scalar.activation(y2[:], bank[:, 0:2 * P], ACT.Identity, bias=ffn_cols[:, 8:9]).then_inc(tr_evac, 1)

            def turn(n):
                first = isinstance(n, int) and n == 0
                last = isinstance(n, int) and n == BODIES - 1
                for s in range(2):
                    more = not (last and s == 1)
                    i1 = 2 * n + s + 1
                    for half in range(2):
                        evac_q(n, s, half)
                        evac_k(n, s, half)
                    if not first:
                        (evac_ffn_columns if s else evac_ffn_tokens)(n)
                    exps(n, s, 0)
                    exps(n, s, 1)
                    if more:
                        evac_v(i1, 1 - s, 0)
                        evac_v(i1, 1 - s, 1)
                    exps(n, s, 2)
                    if more:
                        square(i1, 0)
                    exps(n, s, 3)
                    for c in range(3):
                        if more:
                            square(i1, c + 1)
                        if s and not first:
                            evac_up(n, c)
                    for half in range(2):
                        evac_p(n, s, 2 * half)
                        evac_p(n, s, 2 * half + 1)
                        evac_o(n, s, half)
                    if s:
                        if not first:
                            evac_down(n)
                        evac_wo(n)

            evac_v(0, 0, 0)
            evac_v(0, 0, 1)
            for c in range(4):
                square(0, c)
            over_turns(act, turn)
            evac_ffn_tokens(BODIES)
            evac_ffn_columns(BODIES)
            for j in range(3):
                evac_up(BODIES, j)
            evac_down(BODIES)

        @block.vector
        def _(dve):
            def shift(n, s):
                c = pair_column(n) + s * P
                dve.tensor_scalar(xs[0:64, s, :], xT[0:64, bass.ds(c, P)], 1.0, None, ALU.mult)
                dve.tensor_scalar(xs[64:P, s, :], xT[64:P, bass.ds(c - 1, P)], 1.0, None, ALU.mult).then_inc(xs_done, 1)

            def top_of(n, s, q):
                dve.wait_ge(s_full, 4 * (2 * n + s) + q + 1)
                dve.tensor_reduce(top[:, 4 * q:4 * q + 4], heads4(s_bank(q)), AX_X, ALU.max).then_inc(max_done, 1)

            def subtract_top(n, s, q):
                i = 2 * n + s
                dve.wait_ge(max_done, 4 * i + q + 1)
                wait(dve, exp_done, 4 * (i - 1) + q + 1)
                dve.tensor_tensor(heads4(shifted[:, q, :]), heads4(s_bank(q)), spread(top[:, 4 * q:4 * q + 4], [P, 4, KEYS]),
                                  ALU.subtract).then_inc(s_sub, 1)

            def sums(n, s, q):
                i = 2 * n + s
                dve.wait_ge(exp_done, 4 * i + q + 1)
                dve.tensor_reduce(total[:, 4 * q:4 * q + 4], heads4(probs[:, q, :]), AX_X, ALU.add).then_inc(sum_done, 1)
                dve.wait_ge(sum_done, 4 * i + q + 1)
                wait(dve, probs_normed, 4 * (i - 1) + q + 1)
                dve.reciprocal(rtotal[:, 4 * q:4 * q + 4], total[:, 4 * q:4 * q + 4]).then_inc(rec_done, 1)

            def rotate(i, par, c):
                bank = psum[:, (c + 2) % 3, :].rearrange("p (h d) -> p h d", d=DHEAD)
                t = turn_tables[:, par, :].rearrange("p (f d) -> p f d", f=4)
                cos, sin = t[:, 2 * (c % 2), :], t[:, 2 * (c % 2) + 1, :]
                dve.wait_ge(squared, 4 * i + c + 1)
                if c == 0:
                    dve.wait_ge(tables_done, i + 1)
                wait(dve, qk_normed, 4 * (i - 1) + c + 1)
                straight_c = straight[:, c, :].rearrange("p (h d) -> p h d", d=DHEAD)
                crossed_c = crossed[:, c, :].rearrange("p (h d) -> p h d", d=DHEAD)
                hd = DHEAD // 2
                dve.tensor_tensor(straight_c, bank, cos.unsqueeze(1).broadcast_to([P, 8, DHEAD]), ALU.mult)
                for lo, hi in ((0, hd), (hd, 0)):
                    x = dve.tensor_tensor(crossed_c[:, :, lo:lo + hd], bank[:, :, hi:hi + hd],
                                          sin[:, lo:lo + hd].unsqueeze(1).broadcast_to([P, 8, hd]), ALU.mult)
                x.then_inc(rotary_done, 1)
                wait(dve, newton, STEPS * i)
                dve.tensor_reduce(norm2[:, 8 * c:8 * c + 8], squares[:, c, :].rearrange("p (h d) -> p h d", d=DHEAD),
                                  AX_X, ALU.add).then_inc(norm2_done, 1)

            def norms(i):
                dve.wait_ge(norm2_done, 4 * i + 4)
                wait(dve, qk_normed, 4 * i)
                Rsqrt(dve, newton, STEPS * i, norm2[:], norm2c[:], rnorm[:], na[:], nb[:]).rest()

            def previous_keys(n, s):
                dve.wait_ge(tr_evac, job(n, "AB"[s] + "KT1") + 1)
                keep = 1.0 if s == 0 else inside[:, bass.ds((n + 1) % (TPB // 2), 1)]
                dve.tensor_scalar(kT[:, 1 - s, :, :, 0:WINDOW].rearrange("p j h t -> p (j h) t"),
                                  kT[:, s, :, :, P:P + WINDOW].rearrange("p j h t -> p (j h) t"), keep, None, ALU.mult).then_inc(kprev_done, 1)

            def attention_residual(n):
                c = pair_column(n - 1)
                dve.wait_ge(tr_evac, job(n - 1, "BWO") + 1)
                dve.tensor_tensor(x1T[:, bass.ds(c, 2 * P)], y1[:], xT[:, bass.ds(c, 2 * P)], ALU.add).then_inc(x1_done, 1)
                dve.wait_ge(x1_done, n)
                dve.tensor_scalar(xs2[0:64, :], x1T[0:64, bass.ds(c, 2 * P)], 1.0, None, ALU.mult)
                dve.tensor_scalar(xs2[64:P, :], x1T[64:P, bass.ds(c - 1, 2 * P)], 1.0, None, ALU.mult).then_inc(xs2_done, 1)

            def layernorm_stats(n):
                full = [P, 2, P]
                dve.wait_ge(tr_evac, job(n, "A*XT") + 1)
                dve.tensor_reduce(lmean[:], x_tok[:], AX_X, ALU.add).then_inc(ln_done, 1)
                dve.wait_ge(ln_done, 6 * (n - 1) + 1)
                dve.tensor_scalar(lmean[:], lmean[:], -1.0 / DIM, None, ALU.mult).then_inc(ln_done, 1)
                dve.wait_ge(ln_done, 6 * (n - 1) + 2)
                dve.tensor_tensor(xc_tok[:], x_tok[:], spread(lmean[:], full), ALU.add).then_inc(ln_done, 1)
                dve.wait_ge(ln_done, 6 * (n - 1) + 3)
                dve.tensor_tensor(lsq[:], xc_tok[:], xc_tok[:], ALU.mult).then_inc(ln_done, 1)
                dve.wait_ge(ln_done, 6 * (n - 1) + 4)
                dve.tensor_reduce(norm2[:, 2 * HEADS:], lsq[:], AX_X, ALU.add).then_inc(ln_done, 1)
                dve.wait_ge(ln_done, 6 * (n - 1) + 5)
                dve.tensor_scalar(norm2[:, 2 * HEADS:], norm2[:, 2 * HEADS:], 1.0 / DIM, 1e-5, ALU.mult, ALU.add).then_inc(ln_done, 1)

            def layernorm_apply(n, i):
                dve.wait_ge(newton, STEPS * i + STEPS)
                dve.tensor_tensor(xn_tok[:], xc_tok[:], spread(rnorm[:, 2 * HEADS:], [P, 2, P]), ALU.mult).then_inc(xn_done, 1)

            def gated(n, j):
                m = FFB[j]
                dve.wait_ge(tr_evac, job(n, f"B*H{j}") + 1)
                dve.tensor_tensor(hidden[0:m, j, :], up[0:m, j, :], gate[0:m, j, :], ALU.mult).then_inc(hidden_done, 1)

            def ffn_residual(n):
                c = pair_column(n - 1)
                dve.wait_ge(tr_evac, job(n, "B*FO") + 1)
                dve.tensor_tensor(xT[:, bass.ds(c, 2 * P)], y2[:], x1T[:, bass.ds(c, 2 * P)], ALU.add).then_inc(x2_done, 1)

            def turn(n):
                first = isinstance(n, int) and n == 0
                last = isinstance(n, int) and n == BODIES - 1
                for s in range(2):
                    more = not (last and s == 1)
                    i1 = 2 * n + s + 1
                    ffn = not first
                    if ffn and s == 0:
                        attention_residual(n)
                    for q in range(2):
                        top_of(n, s, q)
                        subtract_top(n, s, q)
                    if ffn and s == 0:
                        layernorm_stats(n)
                    top_of(n, s, 2)
                    subtract_top(n, s, 2)
                    sums(n, s, 0)
                    if more:
                        rotate(i1, 1 - s, 0)
                    top_of(n, s, 3)
                    subtract_top(n, s, 3)
                    sums(n, s, 1)
                    if more:
                        rotate(i1, 1 - s, 1)
                    sums(n, s, 2)
                    if more:
                        rotate(i1, 1 - s, 2)
                    sums(n, s, 3)
                    if ffn and s == 1:
                        gated(n, 0)
                    if more:
                        rotate(i1, 1 - s, 3)
                        previous_keys(n, s)
                    if ffn and s == 1:
                        gated(n, 1)
                    if more:
                        norms(i1)
                    if ffn and s == 0:
                        layernorm_apply(n, i1)
                    if ffn and s == 1:
                        gated(n, 2)
                    if not last:
                        shift(n + 1, s)
                    if ffn and s == 1:
                        ffn_residual(n)

            dve.memset(kT[:], 0.0).then_inc(zeroed, 1)
            dve.memset(v_tok[:], 0.0).then_inc(zeroed, 1)
            dve.memset(norm2[:], 1.0).then_inc(zeroed, 1)
            dve.memset(x1T[:], 0.0).then_inc(zeroed, 1)
            dve.wait_ge(zeroed, 4)
            shift(0, 0)
            shift(0, 1)
            for c in range(4):
                rotate(0, 0, c)
            norms(0)
            over_turns(dve, turn)
            attention_residual(BODIES)
            layernorm_stats(BODIES)
            dve.wait_ge(ln_done, 6 * BODIES)
            Rsqrt(dve, newton, STEPS * 2 * BODIES, norm2[:], norm2c[:], rnorm[:], na[:], nb[:]).rest()
            layernorm_apply(BODIES, 2 * BODIES)
            for j in range(3):
                gated(BODIES, j)
            ffn_residual(BODIES)

        @block.gpsimd
        def _(pool):
            def fold(i, n, s):
                pool.wait_ge(scales_loaded, i // TILES * 16 + 16)
                wait(pool, norm2_done, 4 * (i - 1))
                at = (n % (TPB // 2) * 2 + s) * (4 * DHEAD)
                pool.tensor_tensor(turn_tables[:, s, :], tables[:, bass.ds(at, 4 * DHEAD)], qk_scales[:], ALU.mult).then_inc(tables_done, 1)

            def normalise(n, s, q):
                i = 2 * n + s
                pool.wait_ge(rec_done, 4 * i + q + 1)
                if not (isinstance(i, int) and i == 0):
                    wait(pool, tr_full, (job(n, f"APT{q}") if s else job(n - 1, f"BPT{q}")) + 1)
                pool.tensor_tensor(heads4(probs_n[:, q, :]), heads4(probs[:, q, :]),
                                   spread(rtotal[:, 4 * q:4 * q + 4], [P, 4, KEYS]), ALU.mult).then_inc(probs_normed, 1)

            def add(i, c):
                pool.wait_ge(rotary_done, 4 * i + c + 1)
                pool.tensor_tensor(straight[:, c, :], straight[:, c, :], crossed[:, c, :], ALU.add).then_inc(qk_added, 1)

            def scale(i, c, turned):
                if c == 0:
                    pool.wait_ge(newton, STEPS * i + STEPS)
                    pool.wait_ge(qk_added, 4 * i + 4)
                wait(pool, tr_full, turned)
                pool.tensor_tensor(qk[:, c, :].rearrange("p (h d) -> p h d", d=DHEAD),
                                   straight[:, c, :].rearrange("p (h d) -> p h d", d=DHEAD),
                                   spread(rnorm[:, 8 * c:8 * c + 8], [P, 8, DHEAD]), ALU.mult).then_inc(qk_normed, 1)

            def turn(n):
                last = isinstance(n, int) and n == BODIES - 1
                for s in range(2):
                    more = not (last and s == 1)
                    i1 = 2 * n + s + 1
                    if more:
                        fold(i1, n + s, 1 - s)
                    for q in range(4):
                        normalise(n, s, q)
                        if more:
                            add(i1, q)
                    if more:
                        for c in range(4):
                            scale(i1, c, job(n, "AB"[s] + "KT1") + 1)

            fold(0, 0, 0)
            for c in range(4):
                add(0, c)
            for c in range(4):
                scale(0, c, 0)
            over_turns(pool, turn)


def window_attention(nc, dram, const, base, xT, psum):
    ident, ident16, masks = const["ident"], const["ident16"], const["masks"]
    HD = DIM // HEADS
    BLOCKS = 2 * TILES
    ctx = ExitStack()
    with ctx:
        def sb(n, shape, dt=FP32):
            return ctx.enter_context(nc.sbuf_tensor(f"wa_{n}", shape, dt))

        def sem(n):
            return ctx.enter_context(nc.semaphore(f"wa_{n}"))

        w = sb("w", [P, 4, DIM])
        head_rows = sb("head_rows", [P, HEADS])
        qTall = sb("qTall", [P, TILES * P])
        kTall = sb("kTall", [P, BATCH * PADDED])
        v_win = sb("v_win", [KEYS, BLOCKS, DIM])
        q_heads = sb("q_heads", [P, 2, HEADS, P])
        k_tile = sb("k_tile", [P, 2, WINDOW + P])
        v_tile = sb("v_tile", [KEYS, 2, 2, DIM])
        top = sb("top", [P, HEADS])
        shifted = sb("shifted", [P, 4, QUAD])
        probs = sb("probs", [P, 4, QUAD])
        total, rtotal = sb("total", [P, HEADS]), sb("rtotal", [P, HEADS])
        probs_n = sb("probs_n", [P, 4, QUAD])
        pT = sb("pT", [KEYS, 4, 4 * P])
        o_tok = sb("o_tok", [P, DIM])
        oT = sb("oT", [P, P])

        loaded, kv_full, kv_evac, q_spread = sem("loaded"), sem("kv_full"), sem("kv_evac"), sem("q_spread")
        s_full, max_done, s_sub, exp_done = sem("s_full"), sem("max_done"), sem("s_sub"), sem("exp_done")
        sum_done, rec_done, probs_normed = sem("sum_done"), sem("rec_done"), sem("probs_normed")
        p_turned, p_evac, o_full, o_evac = sem("p_turned"), sem("p_evac"), sem("o_full"), sem("o_evac")
        o_turned, oT_evac, y_full, y_added = sem("o_turned"), sem("oT_evac"), sem("y_full"), sem("y_added")
        k_zeroed = sem("k_zeroed")
        block = ctx.enter_context(nc.Block())

        def s_bank(q):
            return psum[:, q % 2, 0:QUAD]

        GROUPS = 2 * (TILES // 4) + BLOCKS // 4

        @block.sync
        def _(sp):
            sp.dma_start(w[:], dram["Wattn"].rearrange("f p n -> p f n")).then_inc(loaded, 16)
            sp.dma_start(head_rows[:], dram["head_rows"]).then_inc(loaded, 16)

        @block.tensor
        def _(pe):
            pe.wait_ge(loaded, 32)
            for g in range(GROUPS):
                if g >= 8:
                    pe.wait_ge(kv_evac, g - 7)
                if g < 8:
                    c = pair_column(2 * (g % 4))
                    nc.tensor.matmul(psum[:, g % 8, :], w[:, g // 4, :], xT[:, c:c + 4 * P], start=True, stop=True).then_inc(kv_full, 1)
                else:
                    for j in range(4):
                        b = 4 * (g - 8) + j
                        c = pair_column(b // 4) + b % 4 * 64 - WINDOW
                        last = nc.tensor.matmul(psum[0:KEYS, g % 8, j * P:(j + 1) * P], xT[:, c:c + KEYS], w[:, 2, :],
                                                start=True, stop=True, skip_group_check=True)
                    last.then_inc(kv_full, 1)
            pe.wait_ge(kv_evac, GROUPS)

            def scores(t, s, q):
                wait(pe, s_sub, 4 * t + q - 1)
                pe.wait_ge(q_spread, t + 1)
                mask = masks[:, bass.ds(t // 2 % (TPB // 2) * QUAD, QUAD)] if s == 0 else masks[:, QUAD:2 * QUAD]
                nc.tensor.matmul(s_bank(q), ident16[:], mask, start=True, stop=False, skip_group_check=True)
                for h in range(4):
                    for b in range(2):
                        last = nc.tensor.matmul(s_bank(q)[64 * b:64 * b + 64, h * KEYS:(h + 1) * KEYS],
                                                q_heads[:, s, 4 * q + h, 64 * b:64 * b + 64],
                                                k_tile[:, s, 64 * b:64 * b + KEYS], start=False, stop=True, skip_group_check=True)
                last.then_inc(s_full, 1)

            def turn_probs(t, q):
                wait(pe, p_evac, 4 * t + q - 1)
                pe.wait_ge(probs_normed, 4 * t + q + 1)
                for h in range(4):
                    last = nc.tensor.transpose(psum[0:KEYS, 2 + q % 2, h * P:(h + 1) * P], probs_n[:, q, h * KEYS:(h + 1) * KEYS], ident[:])
                last.then_inc(p_turned, 1)

            def tile(t, s):
                scores(t, s, 0)
                scores(t, s, 1)
                scores(t, s, 2)
                turn_probs(t, 0)
                scores(t, s, 3)
                for q in range(1, 4):
                    turn_probs(t, q)
                wait(pe, o_evac, t)
                pe.wait_ge(p_evac, 4 * t + 4)
                for h in range(HEADS):
                    for b in range(2):
                        last = nc.tensor.matmul(psum[64 * b:64 * b + 64, 4, h * HD:(h + 1) * HD],
                                                pT[:, h // 4, h % 4 * P + 64 * b:h % 4 * P + 64 * b + 64],
                                                v_tile[:, s, b, h * HD:(h + 1) * HD],
                                                start=True, stop=True, skip_group_check=True)
                last.then_inc(o_full, 1)
                pe.wait_ge(o_evac, t + 1)
                wait(pe, oT_evac, t)
                nc.tensor.transpose(psum[:, 5, 0:P], o_tok[:], ident[:]).then_inc(o_turned, 1)
                pe.wait_ge(oT_evac, t + 1)
                wait(pe, y_added, t)
                nc.tensor.matmul(psum[:, 6, 0:DIM], oT[:], w[:, 3, :], start=True, stop=True).then_inc(y_full, 1)

            tile(0, 0)
            tile(1, 1)
            with pe.Fori(1, TILES // 2) as p:
                tile(2 * p, 0)
                tile(2 * p + 1, 1)

        @block.scalar
        def _(act):
            act.wait_ge(k_zeroed, 1)
            for g in range(GROUPS):
                act.wait_ge(kv_full, g + 1)
                if g < 4:
                    nc.scalar.activation(qTall[:, 4 * P * g:4 * P * (g + 1)], psum[:, g, :], ACT.Copy, scale=1.0 / float(np.sqrt(HD))).then_inc(kv_evac, 1)
                elif g < 8:
                    c = pair_column(2 * (g - 4))
                    nc.scalar.activation(kTall[:, c:c + 4 * P], psum[:, g, :], ACT.Copy).then_inc(kv_evac, 1)
                else:
                    nc.scalar.activation(v_win[:, 4 * (g - 8):4 * (g - 7), :], psum[0:KEYS, g % 8, :].rearrange("p (j d) -> p j d", j=4), ACT.Copy).then_inc(kv_evac, 1)

            def exps(t, q):
                act.wait_ge(s_sub, 4 * t + q + 1)
                wait(act, probs_normed, 4 * (t - 1) + q + 1)
                nc.scalar.activation(probs[:, q, :], shifted[:, q, :], ACT.Exp).then_inc(exp_done, 1)

            def evac_p(t, q):
                act.wait_ge(p_turned, 4 * t + q + 1)
                nc.scalar.activation(pT[:, q, :], psum[0:KEYS, 2 + q % 2, :], ACT.Copy).then_inc(p_evac, 1)

            def tile(t):
                exps(t, 0)
                exps(t, 1)
                exps(t, 2)
                wait(act, o_full, t)
                evac_p(t, 0)
                exps(t, 3)
                for q in range(1, 4):
                    evac_p(t, q)
                act.wait_ge(o_full, t + 1)
                nc.scalar.activation(o_tok[:], psum[:, 4, 0:P], ACT.Copy).then_inc(o_evac, 1)
                act.wait_ge(o_turned, t + 1)
                nc.scalar.activation(oT[:], psum[:, 5, 0:P], ACT.Copy).then_inc(oT_evac, 1)

            tile(0)
            with act.Fori(1, TILES) as t:
                tile(t)

        @block.vector
        def _(dve):
            dve.memset(kTall[:], 0.0).then_inc(k_zeroed, 1)

            def top_and_shift(t, q):
                dve.wait_ge(s_full, 4 * t + q + 1)
                dve.tensor_reduce(top[:, 4 * q:4 * q + 4], heads4(s_bank(q)), AX_X, ALU.max).then_inc(max_done, 1)
                dve.wait_ge(max_done, 4 * t + q + 1)
                wait(dve, exp_done, 4 * (t - 1) + q + 1)
                dve.tensor_tensor(heads4(shifted[:, q, :]), heads4(s_bank(q)), spread(top[:, 4 * q:4 * q + 4], [P, 4, KEYS]),
                                  ALU.subtract).then_inc(s_sub, 1)

            def sums(t, q):
                dve.wait_ge(exp_done, 4 * t + q + 1)
                dve.tensor_reduce(total[:, 4 * q:4 * q + 4], heads4(probs[:, q, :]), AX_X, ALU.add).then_inc(sum_done, 1)
                dve.wait_ge(sum_done, 4 * t + q + 1)
                wait(dve, probs_normed, 4 * (t - 1) + q + 1)
                dve.reciprocal(rtotal[:, 4 * q:4 * q + 4], total[:, 4 * q:4 * q + 4]).then_inc(rec_done, 1)

            def tile(t):
                top_and_shift(t, 0)
                top_and_shift(t, 1)
                sums(t, 0)
                top_and_shift(t, 2)
                sums(t, 1)
                top_and_shift(t, 3)
                sums(t, 2)
                sums(t, 3)
                dve.wait_ge(y_full, t + 1)
                row = base[:, bass.ds(t, 1), :].rearrange("p o d -> p (o d)")
                dve.tensor_tensor(row, psum[:, 6, 0:DIM], row, ALU.add).then_inc(y_added, 1)

            tile(0)
            with dve.Fori(1, TILES) as t:
                tile(t)

        @block.gpsimd
        def _(pool):
            def q_by_head(t, s):
                pool.wait_ge(kv_evac, GROUPS)
                wait(pool, o_full, t - 1)
                pool.tensor_copy(k_tile[:, s, :], kTall[:, bass.ds(pair_column(t // 2) + s * P - WINDOW, WINDOW + P)])
                pool.tensor_copy(v_tile[:, s, :, :], v_win[:, bass.ds(2 * t, 2), :])
                q_t = qTall[:, bass.ds(t * P, P)]
                pool.tensor_tensor(q_heads[:, s, :, :], q_t.unsqueeze(1).broadcast_to([P, HEADS, P]),
                                   spread(head_rows[:], [P, HEADS, P]), ALU.mult).then_inc(q_spread, 1)

            def normalise(t, q):
                pool.wait_ge(rec_done, 4 * t + q + 1)
                wait(pool, p_turned, 4 * (t - 1) + q + 1)
                pool.tensor_tensor(heads4(probs_n[:, q, :]), heads4(probs[:, q, :]),
                                   spread(rtotal[:, 4 * q:4 * q + 4], [P, 4, KEYS]), ALU.mult).then_inc(probs_normed, 1)

            pool.wait_ge(loaded, 32)
            q_by_head(0, 0)
            q_by_head(1, 1)
            for q in range(4):
                normalise(0, q)
            with pool.Fori(1, TILES // 2) as p:
                q_by_head(2 * p, 0)
                for q in range(4):
                    normalise(2 * p - 1, q)
                q_by_head(2 * p + 1, 1)
                for q in range(4):
                    normalise(2 * p, q)
            for q in range(4):
                normalise(TILES - 1, q)


def macaron(nc, dram, out):
    ctx = ExitStack()
    with ctx:
        def sb(n, shape, dt=FP32):
            return ctx.enter_context(nc.sbuf_tensor(n, shape, dt))

        base = sb("base", [P, TILES, DIM])
        xT = sb("xT", [P, BATCH * PADDED])
        const = {
            "ident": sb("ident", [P, P]), "ident16": sb("ident16", [P, P], BF16),
            "masks": sb("masks", [P, TPB // 2 * QUAD], BF16), "tables": sb("tables", [P, TPB * 4 * DHEAD]),
            "inside": sb("inside", [P, TPB // 2]),
        }
        psum = ctx.enter_context(nc.psum_tensor("psum", [P, 8, 512], FP32))

        with ExitStack() as load:
            arrived = load.enter_context(nc.semaphore("arrived"))
            cleared = load.enter_context(nc.semaphore("cleared"))
            block = load.enter_context(nc.Block())

            @block.sync
            def _(sp):
                sp.dma_start(base[:], dram["x"].rearrange("t p d -> p t d")).then_inc(arrived, 16)
                for n, t in const.items():
                    sp.dma_start(t[:], dram[n]).then_inc(arrived, 16)
                sp.wait_ge(arrived, 16 * (1 + len(const)))

            @block.vector
            def _(dve):
                dve.memset(xT[:], 0.0).then_inc(cleared, 1)
                dve.wait_ge(cleared, 1)

        layernorm_to_columns(nc, base, xT, const["ident"], psum, "ln1")
        stack(nc, dram, const, xT, psum, "f1")
        add_half_of_columns(nc, base, xT, const["ident"], psum, "r1")
        layernorm_to_columns(nc, base, xT, const["ident"], psum, "ln2")
        window_attention(nc, dram, const, base, xT, psum)
        layernorm_to_columns(nc, base, xT, const["ident"], psum, "ln3")
        stack(nc, dram, const, xT, psum, "f2")
        add_half_of_columns(nc, base, xT, const["ident"], psum, "r2")

        with ExitStack() as store:
            stored = store.enter_context(nc.semaphore("stored"))
            block = store.enter_context(nc.Block())

            @block.sync
            def _(sp):
                sp.dma_start(out.rearrange("t p d -> p t d"), base[:]).then_inc(stored, 16)
                sp.wait_ge(stored, 16)


def rotary_constants():
    f = np.float32
    half = np.arange(0, DHEAD, 2, dtype=f)
    inv_freq = (f(1.0) / f(10000.0) ** (half / f(DHEAD))).astype(f)
    t = np.arange(SEQ, dtype=f)
    freqs = (t[:, None] * inv_freq[None, :]).astype(f)
    freqs = np.concatenate([freqs, freqs], -1)
    base_scale = (half + f(0.4 * DHEAD)) / f(1.4 * DHEAD)
    power = (t - SEQ // 2) / f(WINDOW // 2)
    scale = (base_scale[None, :].astype(f) ** power[:, None].astype(f)).astype(f)
    scale = np.concatenate([scale, scale], -1)
    sign = np.where(np.arange(DHEAD) < DHEAD // 2, f(-1), f(1))
    cos, sin = np.cos(freqs), np.sin(freqs) * sign
    inv = f(1.0) / scale
    table = np.stack([cos * scale, sin * scale, cos * inv, sin * inv], 1).astype(f)
    return np.ascontiguousarray(table.reshape(TPB, P, 4 * DHEAD).transpose(1, 0, 2).reshape(P, -1))


def mask_constants():
    q = np.arange(P)[:, None] % 64
    k = np.arange(KEYS)[None, :]
    plain = np.where((k >= q) & (k <= q + WINDOW), 0.0, MASKED)
    start = np.where((np.arange(P)[:, None] < 64) & (k < WINDOW), MASKED, plain)
    rows = [np.tile(start, (1, 4))] + [np.tile(plain, (1, 4))] * (TPB // 2 - 1)
    return np.concatenate(rows, 1)


def kernel(L0_attn_x, L0_attn_Wq, L0_attn_Wk, L0_attn_Wv, L0_attn_Wo, L0_ffn_Wqkv, L0_ffn_q_scale,
           L0_ffn_k_scale, L0_ffn_Wo, L0_ffn_ln_g, L0_ffn_ln_b, L0_ffn_W1, L0_ffn_b1, L0_ffn_W2, L0_ffn_b2):
    import concourse.bacc as bacc
    import ml_dtypes
    from concourse.bass_utils import run_bass_kernel_spmd

    a = lambda x: np.ascontiguousarray(np.asarray(x))
    hd = DHEAD // 2
    qs, ks = a(L0_ffn_q_scale), a(L0_ffn_k_scale)
    swap = lambda s: np.concatenate([s[:, hd:], s[:, :hd]], 1)
    scales = np.concatenate([qs, swap(qs), ks, swap(ks)], 1)
    b1 = a(L0_ffn_b1)
    cols = np.zeros((DEPTH, P, 9), np.float32)
    cols[:, :, 0], cols[:, :, 1], cols[:, :, 8] = a(L0_ffn_ln_g), a(L0_ffn_ln_b), a(L0_ffn_b2)
    for part in range(2):
        for j, m in enumerate(FFB):
            cols[:, :m, 2 + 3 * part + j] = b1[:, part * FF + j * P:part * FF + j * P + m]
    arrays = {
        "x": a(L0_attn_x).reshape(TILES, P, DIM),
        "Wattn": np.stack([a(w).T for w in (L0_attn_Wq, L0_attn_Wk, L0_attn_Wv, L0_attn_Wo)]),
        "Wqkv": a(L0_ffn_Wqkv), "Wo": a(L0_ffn_Wo), "W1": a(L0_ffn_W1), "W2": a(L0_ffn_W2),
        "qk_scales": np.ascontiguousarray(np.broadcast_to(scales[:, None, :], (DEPTH, P, 4 * DHEAD))),
        "ffn_cols": cols,
        "ident": np.eye(P, dtype=np.float32), "ident16": np.eye(P).astype(ml_dtypes.bfloat16),
        "masks": mask_constants().astype(ml_dtypes.bfloat16), "tables": rotary_constants(),
        "inside": np.tile(np.arange(TPB // 2) > 0, (P, 1)).astype(np.float32),
        "head_rows": (np.arange(P)[:, None] // (DIM // HEADS) == np.arange(HEADS)[None, :]).astype(np.float32),
    }
    nc = bacc.Bacc("TRN2", target_bir_lowering=False, num_devices=1)
    dram = {n: nc.dram_tensor(f"in_{n}", v.shape, mybir.dt.from_np(v.dtype), kind="ExternalInput").ap() for n, v in arrays.items()}
    out = nc.dram_tensor("out", (TILES, P, DIM), FP32, kind="ExternalOutput").ap()
    macaron(nc, dram, out)
    r = run_bass_kernel_spmd(nc, [{f"in_{n}": v for n, v in arrays.items()}], core_ids=[0])
    return r.results[0]["out"].reshape(BATCH, SEQ, DIM)
```

```python
from contextlib import ExitStack

import numpy as np

import concourse.bass as bass
from concourse import mybir

FP32 = mybir.dt.float32
BF16 = mybir.dt.bfloat16
INT32 = mybir.dt.int32
ALU = mybir.AluOpType
ACT = mybir.ActivationFunctionType
AX_X = mybir.AxisListType.X

P = 128
BATCH, SEQ, DIM = 2, 1024, 128
DEPTH, HEADS, DHEAD = 6, 16, 64
WINDOW = 32
INNER = HEADS * DHEAD
FF = int(DIM * 4 * 2 / 3)
FFB = [P, P, FF - 2 * P]
TILES = BATCH * SEQ // P
PAIRS = TILES // 2
TPB = SEQ // P
PADDED = WINDOW + SEQ
KEYS = 64 + WINDOW
QUAD = 4 * KEYS
BODIES = DEPTH * PAIRS
MASKED = -1.0e30
RSQRT_MAGIC = float(0x5F3759DF)
STEPS = 11
CHUNKS = ["q0", "k0", "v0", "q1", "k1", "v1"]
TURN_A = ["*QT1", "*KT1", "*PT0", "*PT1", "*OT0", "*PT2", "QT0", "*PT3", "KT0", "*OT1", "*WO"]
TURN_B = ["QT1", "*XT", "KT1", "PT0", "PT1", "OT0", "*XN", "PT2", "QT0", "KT0", "*H0", "*H1", "PT3", "*H2",
          "OT1", "*FO"]
TURN = ["A" + x for x in TURN_A] + ["B" + x for x in TURN_B]
FIRST_TURN = [x for x in TURN if "*" not in x]
REST = [x for x in TURN if "*" in x]
SKIPPED = len(TURN) - len(FIRST_TURN)


def job(n, name):
    if isinstance(n, int) and n == 0:
        return FIRST_TURN.index(name)
    if isinstance(n, int) and n == BODIES:
        return len(TURN) * BODIES - SKIPPED + REST.index(name)
    return n * len(TURN) + (TURN.index(name) - SKIPPED)


def bank_of(n, name):
    if isinstance(n, int):
        return 5 + job(n, name) % 3
    return 5 + (TURN.index(name) - SKIPPED) % 3


assert len(TURN) % 3 == 0


def of_tile_before(s, name):
    return "B" + name if s else "A*" + name


def wait(eng, sem, value):
    if not (isinstance(value, int) and value <= 0):
        eng.wait_ge(sem, value)


def known(eng, value):
    return value if isinstance(value, int) else eng.snap(value)


def pair_column(n):
    p = n % PAIRS
    return p * (2 * P) + p // (PAIRS // 2) * WINDOW + WINDOW


def over_turns(eng, body):
    body(0)
    with eng.Fori(1, BODIES - 1) as n:
        body(n)
    body(BODIES - 1)
    body(BODIES)


def has_pair(n):
    return not (isinstance(n, int) and n == BODIES)


def has_before(n):
    return not (isinstance(n, int) and n == 0)


def has_next(n):
    return not (isinstance(n, int) and n >= BODIES - 1)


def heads4(ap):
    return ap.rearrange("p (h k) -> p h k", h=4)


def spread(ap, shape):
    return ap.unsqueeze(2).broadcast_to(shape)


class Rsqrt:

    def __init__(self, eng, done, count, x, xc, y, a, b):
        self.eng, self.done, self.count = eng, done, count
        self.x, self.xc, self.y, self.a, self.b = x, xc, y, a, b
        self.k = 0

    def step(self):
        e, k = self.eng, self.k
        if k:
            e.wait_ge(self.done, self.count + k)
        if k == 0:
            i = e.tensor_scalar(self.xc, self.x, 1e-24, None, ALU.max)
        elif k == 1:
            i = e.tensor_scalar(self.y.bitcast(INT32), self.xc.bitcast(INT32), -0.5, RSQRT_MAGIC, ALU.mult, ALU.add)
        elif k % 3 == 2:
            i = e.scalar_tensor_tensor(self.a, self.y, -0.5, self.y, ALU.mult, ALU.mult)
        elif k % 3 == 0:
            i = e.tensor_tensor(self.b, self.a, self.xc, ALU.mult)
        else:
            i = e.scalar_tensor_tensor(self.y, self.b, 1.5, self.y, ALU.add, ALU.mult)
        i.then_inc(self.done, 1)
        self.k += 1

    def steps(self, count):
        for _ in range(count):
            self.step()


def layernorm_to_columns(nc, base, xT, ident, psum, name):
    with ExitStack() as ctx:
        sb = lambda n, s: ctx.enter_context(nc.sbuf_tensor(f"{name}_{n}", s, FP32))
        sem = lambda n: ctx.enter_context(nc.semaphore(f"{name}_{n}"))
        centred, square = sb("centred", [P, TILES, DIM]), sb("square", [P, TILES, DIM])
        mean, var, varc = sb("mean", [P, TILES]), sb("var", [P, TILES]), sb("varc", [P, TILES])
        rstd, ta, tb = sb("rstd", [P, TILES]), sb("ta", [P, TILES]), sb("tb", [P, TILES])
        stats, newton, normed, turned, evacuated = (sem(x) for x in ("stats", "newton", "normed", "turned", "evacuated"))
        block = ctx.enter_context(nc.Block())

        @block.vector
        def _(dve):
            full = [P, TILES, DIM]
            dve.tensor_reduce(mean[:], base[:], AX_X, ALU.add).then_inc(stats, 1)
            dve.wait_ge(stats, 1)
            dve.tensor_scalar(mean[:], mean[:], -1.0 / DIM, None, ALU.mult).then_inc(stats, 1)
            dve.wait_ge(stats, 2)
            dve.tensor_tensor(centred[:], base[:], spread(mean[:], full), ALU.add).then_inc(stats, 1)
            dve.wait_ge(stats, 3)
            dve.tensor_tensor(square[:], centred[:], centred[:], ALU.mult).then_inc(stats, 1)
            dve.wait_ge(stats, 4)
            dve.tensor_reduce(var[:], square[:], AX_X, ALU.add).then_inc(stats, 1)
            dve.wait_ge(stats, 5)
            dve.tensor_scalar(var[:], var[:], 1.0 / DIM, 1e-5, ALU.mult, ALU.add).then_inc(stats, 1)
            dve.wait_ge(stats, 6)
            Rsqrt(dve, newton, 0, var[:], varc[:], rstd[:], ta[:], tb[:]).steps(STEPS)
            dve.wait_ge(newton, STEPS)
            dve.tensor_tensor(centred[:], centred[:], spread(rstd[:], full), ALU.mult).then_inc(normed, 1)

        @block.tensor
        def _(pe):
            pe.wait_ge(normed, 1)
            for t in range(TILES):
                last = nc.tensor.transpose(psum[:, t // 4, t % 4 * P:(t % 4 + 1) * P], centred[:, t, :], ident[:])
                if t % 4 == 3:
                    last.then_inc(turned, 1)

        @block.scalar
        def _(act):
            for g in range(TILES // 4):
                act.wait_ge(turned, g + 1)
                c = pair_column(2 * g)
                nc.scalar.activation(xT[:, c:c + 4 * P], psum[:, g, :], ACT.Copy).then_inc(evacuated, 1)


def add_half_of_columns(nc, base, xT, ident, psum, name):
    with ExitStack() as ctx:
        sem = lambda n: ctx.enter_context(nc.semaphore(f"{name}_{n}"))
        turned, added = sem("turned"), sem("added")
        block = ctx.enter_context(nc.Block())

        @block.tensor
        def _(pe):
            for t in range(TILES):
                c = pair_column(t // 2) + t % 2 * P
                last = nc.tensor.transpose(psum[:, t // 4, t % 4 * P:(t % 4 + 1) * P], xT[:, c:c + P], ident[:])
                if t % 4 == 3:
                    last.then_inc(turned, 1)

        @block.vector
        def _(dve):
            for g in range(TILES // 4):
                dve.wait_ge(turned, g + 1)
                tiles = base[:, 4 * g:4 * g + 4, :].rearrange("p t d -> p (t d)")
                dve.scalar_tensor_tensor(tiles, psum[:, g, :], 0.5, tiles, ALU.mult, ALU.add).then_inc(added, 1)


def stack(nc, dram, const, xT, psum, name):
    ident, ident16, masks, tables = const["ident"], const["ident16"], const["masks"], const["tables"]
    inside = const["inside"]
    ctx = ExitStack()
    with ctx:
        def sb(n, shape, dt=FP32):
            return ctx.enter_context(nc.sbuf_tensor(f"{name}_{n}", shape, dt))

        def sem(n):
            return ctx.enter_context(nc.semaphore(f"{name}_{n}"))

        w_qkv = sb("w_qkv", [P, 3 * INNER])
        w_o = sb("w_o", [P, INNER // P, DIM])
        w_1 = sb("w_1", [P, 2 * FF])
        w_2 = sb("w_2", [P, 3, DIM])
        ffn_cols = sb("ffn_cols", [P, 9])
        qk_scales = sb("qk_scales", [P, 4 * DHEAD])
        x1T = sb("x1T", [P, BATCH * PADDED])
        xs = sb("xs", [P, 2, P])
        turn_tables = sb("turn_tables", [P, 2, 4 * DHEAD])
        squares = sb("squares", [P, 4, 512])
        norm2 = sb("norm2", [P, 2 * HEADS])
        norm2c = sb("norm2c", [P, 2 * HEADS])
        rnorm = sb("rnorm", [P, 2 * HEADS])
        na, nb = sb("na", [P, 2 * HEADS]), sb("nb", [P, 2 * HEADS])
        straight = sb("straight", [P, 4, 512])
        crossed = sb("crossed", [P, 4, 512])
        qk = sb("qk", [P, 4, 512])
        qT = sb("qT", [P, 8, P])
        kT = sb("kT", [P, 2, 8, 2, WINDOW + P])
        v_tok = sb("v_tok", [P, 2, INNER])
        v_win = sb("v_win", [KEYS, 2, 2, INNER])
        neg_top = sb("neg_top", [P, HEADS])
        probs = sb("probs", [P, 4, QUAD])
        total, rtotal = sb("total", [P, HEADS]), sb("rtotal", [P, HEADS])
        probs_n = sb("probs_n", [P, 4, QUAD])
        pT = sb("pT", [KEYS, 4, 4 * P])
        oT = sb("oT", [P, 8, 2 * P])
        y1 = sb("y1", [P, 2 * P])
        xs2 = sb("xs2", [P, 2 * P])
        x_tok = sb("x_tok", [P, 2, P])
        lmean, nmean, lvar, lvare, lvarc, rstd, la, lb = (sb(x, [P, 2]) for x in ("lmean", "nmean", "lvar", "lvare", "lvarc", "rstd", "la", "lb"))
        lsq = sb("lsq", [P, 2, P])
        xn_tok = sb("xn_tok", [P, 2, P])
        xnT = sb("xnT", [P, 2 * P])
        up = sb("up", [P, 3, 2 * P])
        gate = sb("gate", [P, 3, 2 * P])
        hidden = sb("hidden", [P, 3, 2 * P])
        y2 = sb("y2", [P, 2 * P])

        proj_full, s_full, tr_full, wo_begun = sem("proj_full"), sem("s_full"), sem("tr_full"), sem("wo_begun")
        tr_evac, v_evac, squared, exp_done = sem("tr_evac"), sem("v_evac"), sem("squared"), sem("exp_done")
        ln_squared = sem("ln_squared")
        zeroed = sem("zeroed")
        xs_done, max_done, rec_done = (sem(x) for x in ("xs_done", "max_done", "rec_done"))
        rotary_done, norm2_done, newton, k_normed = sem("rotary_done"), sem("norm2_done"), sem("newton"), sem("k_normed")
        x1_begun = sem("x1_begun")
        kprev_done, x1_done, xs2_done, ln_done, xn_done = (sem(x) for x in ("kprev_done", "x1_done", "xs2_done", "ln_done", "xn_done"))
        hidden_done, x2_done, ln_newton = sem("hidden_done"), sem("x2_done"), sem("ln_newton")
        tables_done, probs_normed, qk_added, q_normed = (sem(x) for x in ("tables_done", "probs_normed", "qk_added", "q_normed"))
        loaded = [sem("first_heads_loaded"), sem("last_heads_loaded")]
        scales_loaded, wo_loaded, ffn_loaded, v_moved = (sem(x) for x in ("scales_loaded", "wo_loaded", "ffn_loaded", "v_moved"))

        block = ctx.enter_context(nc.Block())

        def s_bank(q):
            return psum[:, 3 + q % 2, 0:QUAD]

        @block.sync
        def _(sp):
            def load_half(l, half):
                if not (isinstance(l, int) and l == 0):
                    sp.wait_ge(proj_full, known(sp, 6 * TILES * l - 3 + 3 * half))
                view = lambda ap: ap.rearrange("p (t h n) -> p t h n", t=3, h=2)[:, :, half, :]
                sp.dma_start(view(w_qkv[:]), view(dram["Wqkv"][bass.ds(l, 1), :, :].rearrange("o p n -> (o p) n"))).then_inc(loaded[half], 16)

            def load_scales(l):
                wait(sp, tables_done, known(sp, TILES * l))
                sp.dma_start(qk_scales[:], dram["qk_scales"][bass.ds(l, 1), :, :].rearrange("o p n -> p (o n)")).then_inc(scales_loaded, 16)

            def load_wo(l):
                if not (isinstance(l, int) and l == 0):
                    wait(sp, tr_full, known(sp, job(PAIRS * l, "A*WO") + 1))
                sp.dma_start(w_o[:], dram["Wo"][bass.ds(l, 1), :, :].rearrange("o (j p) n -> p (o j) n", p=P)).then_inc(wo_loaded, 16)

            def load_ffn(l):
                wait(sp, x2_done, known(sp, PAIRS * l))
                sp.dma_start(w_1[:], dram["W1"][bass.ds(l, 1), :, :].rearrange("o p n -> p (o n)")).then_inc(ffn_loaded, 16)
                sp.dma_start(w_2[:, 0:2, :], dram["W2"][bass.ds(l, 1), 0:2 * P, :].rearrange("o (j p) n -> p (o j) n", p=P)).then_inc(ffn_loaded, 16)
                sp.dma_start(w_2[0:FFB[2], 2, :], dram["W2"][bass.ds(l, 1), 2 * P:FF, :].rearrange("o p n -> p (o n)")).then_inc(ffn_loaded, 16)
                sp.dma_start(ffn_cols[:], dram["ffn_cols"][bass.ds(l, 1), :, :].rearrange("o p n -> p (o n)")).then_inc(ffn_loaded, 16)

            def move_v(n, s):
                wait(sp, v_evac, 2 * (2 * n + s) + 2)
                now, before = v_tok[:, s, :], v_tok[:, 1 - s, :]
                sp.dma_start(v_win[0:WINDOW, s, 0, :], before[P - WINDOW:P, :]).then_inc(v_moved, 16)
                sp.dma_start(v_win[WINDOW:KEYS, s, 0, :], now[0:64, :]).then_inc(v_moved, 16)
                sp.dma_start(v_win[:, s, 1, :], now[WINDOW:P, :]).then_inc(v_moved, 16)

            def layer(l, first, last):
                n = PAIRS * l
                move_v(n, 0)
                if not first:
                    load_wo(l)
                move_v(n, 1)
                if not first:
                    load_ffn(l)
                with sp.Fori(1, PAIRS - 1) as p:
                    move_v(n + p, 0)
                    move_v(n + p, 1)
                move_v(n + PAIRS - 1, 0)
                if not last:
                    load_scales(l + 1)
                    load_half(l + 1, 0)
                    load_half(l + 1, 1)
                move_v(n + PAIRS - 1, 1)

            load_half(0, 0)
            load_scales(0)
            load_half(0, 1)
            load_wo(0)
            load_ffn(0)
            sp.wait_ge(zeroed, 2)
            layer(0, True, False)
            with sp.Fori(1, DEPTH - 1) as l:
                layer(l, False, False)
            layer(DEPTH - 1, False, True)

        @block.tensor
        def _(pe):
            def project(i, par, c):
                if c == 0:
                    pe.wait_ge(xs_done, i + 1)
                what, half = CHUNKS[c][0], int(CHUNKS[c][1])
                at = {"q": 0, "k": INNER, "v": 2 * INNER}[what] + 512 * half
                if c == 5 and par == 0 and not (isinstance(i, int) and i == 0):
                    pe.wait_ge(x1_begun, i // 2)
                elif what == "v":
                    wait(pe, v_evac, 2 * i + half)
                else:
                    wait(pe, norm2_done, 4 * i + 2 * half + c % 3 - 1)
                if what == "q":
                    pe.wait_ge(loaded[half], i // TILES * 16 + 16)
                nc.tensor.matmul(psum[:, c % 3, :], xs[:, par, :], w_qkv[:, at:at + 512],
                                 start=True, stop=True).then_inc(proj_full, 1)

            def scores(n, s, q):
                i, par = (2 * n + s, s) if q < 2 else (2 * n + s - 1, 1 - s)
                wait(pe, exp_done, 4 * i + q - 1)
                if q == 0:
                    pe.wait_ge(tr_evac, job(n, "AB"[s] + "KT0") + 1)
                    wait(pe, kprev_done, i)
                if q == 2:
                    pe.wait_ge(tr_evac, job(n, of_tile_before(s, "KT1")) + 1)
                mask = masks[:, bass.ds(n % (TPB // 2) * QUAD, QUAD)] if par == 0 else masks[:, QUAD:2 * QUAD]
                nc.tensor.matmul(s_bank(q), ident16[:], mask, start=True, stop=False, skip_group_check=True)
                for pr in range(2):
                    for b in range(2):
                        last = nc.tensor.matmul(
                            s_bank(q)[64 * b:64 * b + 64, pr * 2 * KEYS:(pr + 1) * 2 * KEYS],
                            qT[:, 2 * q + pr, 64 * b:64 * b + 64], kT[:, par, 2 * q + pr, :, 64 * b:64 * b + KEYS],
                            start=False, stop=True, skip_group_check=True)
                last.then_inc(s_full, 1)

            def tenant(n, name):
                wait(pe, tr_evac, job(n, name) - 2)
                return psum[:, bank_of(n, name), :]

            def turn_qk(n, s, what, half):
                name, i = ("AB"[s] + what + "0", 2 * n + s) if half == 0 else (of_tile_before(s, what + "1"), 2 * n + s - 1)
                bank = tenant(n, name)
                c = 2 * half + "QK".index(what[0])
                pe.wait_ge(q_normed if what[0] == "Q" else k_normed, 2 * i + half + 1)
                for j in range(4):
                    last = nc.tensor.transpose(bank[:, j * P:(j + 1) * P], qk[:, c, j * P:(j + 1) * P], ident[:])
                last.then_inc(tr_full, 1)

            def turn_probs(n, s, q):
                bank = tenant(n, of_tile_before(s, f"PT{q}"))
                pe.wait_ge(probs_normed, 4 * (2 * n + s - 1) + q + 1)
                for h in range(4):
                    last = nc.tensor.transpose(bank[0:KEYS, h * P:(h + 1) * P], probs_n[:, q, h * KEYS:(h + 1) * KEYS], ident[:])
                last.then_inc(tr_full, 1)

            def times_v(n, s, half):
                bank = tenant(n, of_tile_before(s, f"OT{half}"))
                pe.wait_ge(tr_evac, job(n, of_tile_before(s, f"PT{2 * half + 1}")) + 1)
                if half == 0:
                    pe.wait_ge(v_moved, 48 * (2 * n + s))
                for pr in range(4):
                    for b in range(2):
                        for h2 in range(2):
                            h = 8 * half + 2 * pr + h2
                            last = nc.tensor.matmul(
                                bank[64 * h2:64 * h2 + 64, pr * P + 64 * b:pr * P + 64 * b + 64],
                                v_win[:, 1 - s, b, h * DHEAD:(h + 1) * DHEAD],
                                pT[:, h // 4, h % 4 * P + 64 * b:h % 4 * P + 64 * b + 64],
                                start=True, stop=True, skip_group_check=True)
                last.then_inc(tr_full, 1)

            def times_wo(n, half):
                if half == 0:
                    pe.wait_ge(v_evac, 4 * BODIES if isinstance(n, int) and n == BODIES else 4 * n + 1)
                    pe.wait_ge(tr_evac, job(n, "A*OT0") + 1)
                    pe.wait_ge(wo_loaded, (n - 1) // PAIRS * 16 + 16)
                    bank = psum[:, 2, :]
                else:
                    bank = tenant(n, "A*WO")
                    pe.wait_ge(tr_evac, job(n, "A*OT1") + 1)
                for j in range(4 * half, 4 * half + 4):
                    last = nc.tensor.matmul(bank[:, 0:2 * P], w_o[:, j, :], oT[:, j, :], start=(j % 4 == 0), stop=(j % 4 == 3))
                last.then_inc(tr_full if half else wo_begun, 1)

            def ffn_tokens(n):
                bank = tenant(n, "B*XT")
                pe.wait_ge(xs2_done, n)
                for t in range(2):
                    last = nc.tensor.transpose(bank[:, t * P:(t + 1) * P], xs2[:, t * P:(t + 1) * P], ident[:])
                last.then_inc(tr_full, 1)

            def ffn_columns(n):
                bank = tenant(n, "B*XN")
                pe.wait_ge(xn_done, n)
                for t in range(2):
                    last = nc.tensor.transpose(bank[:, t * P:(t + 1) * P], xn_tok[:, t, :], ident[:])
                last.then_inc(tr_full, 1)

            def ffn_up(n, j):
                bank = tenant(n, f"B*H{j}")
                if j == 0:
                    pe.wait_ge(tr_evac, job(n, "B*XN") + 1)
                    pe.wait_ge(ffn_loaded, (n - 1) // PAIRS * 64 + 64)
                m = FFB[j]
                nc.tensor.matmul(bank[0:m, 0:2 * P], w_1[:, j * P:j * P + m], xnT[:], start=True, stop=True, skip_group_check=True)
                nc.tensor.matmul(bank[0:m, 2 * P:4 * P], w_1[:, FF + j * P:FF + j * P + m], xnT[:],
                                 start=True, stop=True, skip_group_check=True).then_inc(tr_full, 1)

            def ffn_down(n):
                bank = tenant(n, "B*FO")
                pe.wait_ge(hidden_done, 3 * n)
                for j, m in enumerate(FFB):
                    last = nc.tensor.matmul(bank[:, 0:2 * P], w_2[0:m, j, :], hidden[0:m, j, :], start=(j == 0), stop=(j == 2))
                last.then_inc(tr_full, 1)

            def turn(n):
                new, old = has_pair(n), has_before(n)
                i = 2 * n
                if old:
                    turn_qk(n, 0, "QT", 1)
                if new:
                    project(i, 0, 0)
                    project(i, 0, 1)
                if old:
                    turn_qk(n, 0, "KT", 1)
                    turn_probs(n, 0, 0)
                if new:
                    project(i, 0, 2)
                if old:
                    turn_probs(n, 0, 1)
                    scores(n, 0, 2)
                if new:
                    project(i, 0, 3)
                if old:
                    scores(n, 0, 3)
                    times_v(n, 0, 0)
                if new:
                    project(i, 0, 4)
                if old:
                    times_wo(n, 0)
                    turn_probs(n, 0, 2)
                if new:
                    turn_qk(n, 0, "QT", 0)
                if old:
                    turn_probs(n, 0, 3)
                if new:
                    project(i, 0, 5)
                    turn_qk(n, 0, "KT", 0)
                if old:
                    times_v(n, 0, 1)
                if new:
                    scores(n, 0, 0)
                    scores(n, 0, 1)
                if old:
                    times_wo(n, 1)
                i = 2 * n + 1
                if new:
                    project(i, 1, 0)
                    project(i, 1, 1)
                    turn_qk(n, 1, "QT", 1)
                if old:
                    ffn_tokens(n)
                if new:
                    project(i, 1, 2)
                    turn_qk(n, 1, "KT", 1)
                    turn_probs(n, 1, 0)
                    project(i, 1, 3)
                    scores(n, 1, 2)
                    turn_probs(n, 1, 1)
                    scores(n, 1, 3)
                    times_v(n, 1, 0)
                    project(i, 1, 4)
                    project(i, 1, 5)
                if old:
                    ffn_columns(n)
                if new:
                    turn_probs(n, 1, 2)
                    turn_qk(n, 1, "QT", 0)
                    turn_qk(n, 1, "KT", 0)
                if old:
                    ffn_up(n, 0)
                    ffn_up(n, 1)
                if new:
                    turn_probs(n, 1, 3)
                    scores(n, 1, 0)
                if old:
                    ffn_up(n, 2)
                if new:
                    scores(n, 1, 1)
                    times_v(n, 1, 1)
                if old:
                    ffn_down(n)

            over_turns(pe, turn)

        @block.scalar
        def _(act):
            def evac(n, name):
                act.wait_ge(tr_full, job(n, name) + 1)
                return psum[:, bank_of(n, name), :]

            def evac_q(n, s, half):
                bank = evac(n, "AB"[s] + "QT0" if half == 0 else of_tile_before(s, "QT1"))
                wait(act, s_full, 4 * (2 * n + s - 1 - half) + 2 * half + 2)
                nc.scalar.activation(qT[:, 4 * half:4 * half + 4, :], bank.rearrange("p (j t) -> p j t", j=4),
                                     ACT.Copy, scale=8.0).then_inc(tr_evac, 1)

            def evac_k(n, s, half):
                bank, par = (evac(n, "AB"[s] + "KT0"), s) if half == 0 else (evac(n, of_tile_before(s, "KT1")), 1 - s)
                bank = bank.rearrange("p (j t) -> p j t", j=4)
                act.wait_ge(zeroed, 2)
                for h2 in range(2):
                    r = slice(64 * h2, 64 * h2 + 64)
                    last = nc.scalar.activation(kT[r, par, 4 * half:4 * half + 4, h2, WINDOW:], bank[r], ACT.Copy)
                last.then_inc(tr_evac, 1)

            def evac_v(i, par, half):
                act.wait_ge(proj_full, 6 * i + 3 * half + 3)
                wait(act, v_moved, 48 * i)
                nc.scalar.activation(v_tok[:, par, 512 * half:512 * half + 512], psum[:, 2, :], ACT.Copy).then_inc(v_evac, 1)

            def square(i, c):
                act.wait_ge(proj_full, 6 * i + c + c // 2 + 1)
                wait(act, norm2_done, 4 * (i - 1) + c + 1)
                nc.scalar.activation(squares[:, c, :], psum[:, c % 2, :], ACT.Square).then_inc(squared, 1)

            def exps(i, q):
                act.wait_ge(max_done, 4 * i + q + 1)
                wait(act, probs_normed, 4 * (i - 1) + q + 1)
                for h in range(4):
                    at, one = slice(h * KEYS, (h + 1) * KEYS), slice(4 * q + h, 4 * q + h + 1)
                    last = nc.scalar.activation(probs[:, q, at], s_bank(q)[:, at], ACT.Exp, bias=neg_top[:, one], accum_out=total[:, one])
                last.then_inc(exp_done, 1)

            def evac_p(n, s, q):
                bank = evac(n, of_tile_before(s, f"PT{q}"))
                nc.scalar.activation(pT[:, q, :], bank[0:KEYS, :], ACT.Copy).then_inc(tr_evac, 1)

            def evac_o(n, s, half):
                bank = evac(n, of_tile_before(s, f"OT{half}"))
                nc.scalar.activation(oT[:, 4 * half:4 * half + 4, (1 - s) * P:(2 - s) * P], bank.rearrange("p (j t) -> p j t", j=4),
                                     ACT.Copy).then_inc(tr_evac, 1)

            def evac_wo(n):
                bank = evac(n, "A*WO")
                wait(act, x1_done, n - 1)
                nc.scalar.activation(y1[:], bank[:, 0:2 * P], ACT.Copy).then_inc(tr_evac, 1)

            def evac_ffn_tokens(n):
                bank = evac(n, "B*XT")
                for t in range(2):
                    last = nc.scalar.activation(x_tok[:, t, :], bank[:, t * P:(t + 1) * P], ACT.Identity, accum_out=lmean[:, t:t + 1])
                last.then_inc(tr_evac, 1)

            def centred_squares(n):
                act.wait_ge(ln_done, 2 * n - 1)
                for t in range(2):
                    last = nc.scalar.activation(lsq[:, t, :], x_tok[:, t, :], ACT.Square, bias=nmean[:, t:t + 1], accum_out=lvar[:, t:t + 1])
                last.then_inc(ln_squared, 1)

            def evac_ffn_columns(n):
                bank = evac(n, "B*XN")
                act.wait_ge(ffn_loaded, (n - 1) // PAIRS * 64 + 64)
                nc.scalar.activation(xnT[:], bank[:, 0:2 * P], ACT.Identity, bias=ffn_cols[:, 1:2], scale=ffn_cols[:, 0:1]).then_inc(tr_evac, 1)

            def evac_up(n, j):
                m = FFB[j]
                bank = evac(n, f"B*H{j}")
                wait(act, hidden_done, 3 * (n - 1))
                nc.scalar.activation(gate[0:m, j, :], bank[0:m, 2 * P:4 * P], ACT.Gelu, bias=ffn_cols[0:m, 5 + j:6 + j])
                nc.scalar.activation(up[0:m, j, :], bank[0:m, 0:2 * P], ACT.Identity, bias=ffn_cols[0:m, 2 + j:3 + j]).then_inc(tr_evac, 1)

            def evac_down(n):
                bank = evac(n, "B*FO")
                wait(act, x2_done, n - 1)
                nc.scalar.activation(y2[:], bank[:, 0:2 * P], ACT.Identity, bias=ffn_cols[:, 8:9]).then_inc(tr_evac, 1)

            def turn(n):
                new, old = has_pair(n), has_before(n)
                i = 2 * n
                if old:
                    evac_q(n, 0, 1)
                if new:
                    square(i, 0)
                if old:
                    evac_k(n, 0, 1)
                if new:
                    square(i, 1)
                if old:
                    evac_p(n, 0, 0)
                if new:
                    evac_v(i, 0, 0)
                if old:
                    evac_p(n, 0, 1)
                    exps(i - 1, 2)
                    evac_o(n, 0, 0)
                    exps(i - 1, 3)
                if new:
                    square(i, 2)
                    square(i, 3)
                if old:
                    evac_p(n, 0, 2)
                if new:
                    evac_q(n, 0, 0)
                if old:
                    evac_p(n, 0, 3)
                if new:
                    evac_k(n, 0, 0)
                if old:
                    evac_o(n, 0, 1)
                if new:
                    evac_v(i, 0, 1)
                    exps(i, 0)
                    exps(i, 1)
                if old:
                    evac_wo(n)
                i = 2 * n + 1
                if new:
                    square(i, 0)
                    square(i, 1)
                    evac_q(n, 1, 1)
                if old:
                    evac_ffn_tokens(n)
                if new:
                    evac_k(n, 1, 1)
                if old:
                    centred_squares(n)
                if new:
                    square(i, 2)
                    evac_p(n, 1, 0)
                    evac_p(n, 1, 1)
                    evac_v(i, 1, 0)
                    exps(i - 1, 2)
                    exps(i - 1, 3)
                    evac_o(n, 1, 0)
                    square(i, 3)
                if old:
                    evac_ffn_columns(n)
                if new:
                    evac_p(n, 1, 2)
                    evac_q(n, 1, 0)
                    evac_k(n, 1, 0)
                if old:
                    evac_up(n, 0)
                    evac_up(n, 1)
                if new:
                    evac_p(n, 1, 3)
                if old:
                    evac_up(n, 2)
                if new:
                    exps(i, 0)
                    evac_v(i, 1, 1)
                    evac_o(n, 1, 1)
                if old:
                    evac_down(n)
                if new:
                    exps(i, 1)

            over_turns(act, turn)

        @block.vector
        def _(dve):
            def shift(n, s):
                c = pair_column(n) + s * P
                dve.tensor_scalar(xs[0:64, s, :], xT[0:64, bass.ds(c, P)], 1.0, None, ALU.mult)
                dve.tensor_scalar(xs[64:P, s, :], xT[64:P, bass.ds(c - 1, P)], 1.0, None, ALU.mult).then_inc(xs_done, 1)

            def top_of(i, q):
                dve.wait_ge(s_full, 4 * i + q + 1)
                dve.tensor_reduce(neg_top[:, 4 * q:4 * q + 4], heads4(s_bank(q)), AX_X, ALU.max, negate=True).then_inc(max_done, 1)

            def invert_sum(i, q):
                dve.wait_ge(exp_done, 4 * i + q + 1)
                wait(dve, probs_normed, 4 * (i - 1) + q + 1)
                dve.reciprocal(rtotal[:, 4 * q:4 * q + 4], total[:, 4 * q:4 * q + 4]).then_inc(rec_done, 1)

            def rotate(i, par, c, between=lambda count: None):
                bank = psum[:, c % 2, :].rearrange("p (h d) -> p h d", d=DHEAD)
                t = turn_tables[:, par, :].rearrange("p (f d) -> p f d", f=4)
                cos, sin = t[:, 2 * (c % 2), :], t[:, 2 * (c % 2) + 1, :]
                dve.wait_ge(squared, 4 * i + c + 1)
                if c == 0:
                    dve.wait_ge(tables_done, i + 1)
                wait(dve, (q_normed, k_normed)[c % 2], 2 * (i - 1) + c // 2 + 1)
                straight_c = straight[:, c, :].rearrange("p (h d) -> p h d", d=DHEAD)
                crossed_c = crossed[:, c, :].rearrange("p (h d) -> p h d", d=DHEAD)
                hd = DHEAD // 2
                dve.tensor_tensor(straight_c, bank, cos.unsqueeze(1).broadcast_to([P, 8, DHEAD]), ALU.mult)
                between(1)
                for lo, hi in ((0, hd), (hd, 0)):
                    x = dve.tensor_tensor(crossed_c[:, :, lo:lo + hd], bank[:, :, hi:hi + hd],
                                          sin[:, lo:lo + hd].unsqueeze(1).broadcast_to([P, 8, hd]), ALU.mult)
                x.then_inc(rotary_done, 1)
                between(1)
                wait(dve, newton, STEPS * (2 * (i - 1) + c // 2 + 1))
                dve.tensor_reduce(norm2[:, 8 * c:8 * c + 8], squares[:, c, :].rearrange("p (h d) -> p h d", d=DHEAD),
                                  AX_X, ALU.add).then_inc(norm2_done, 1)

            def norms(i, half):
                dve.wait_ge(norm2_done, 4 * i + 2 * half + 2)
                at = slice(HEADS * half, HEADS * half + HEADS)
                return Rsqrt(dve, newton, STEPS * (2 * i + half), norm2[:, at], norm2c[:, at], rnorm[:, at], na[:, at], nb[:, at])

            def scale_k(i, half):
                c = 2 * half + 1
                dve.wait_ge(newton, STEPS * (2 * i + half + 1))
                dve.wait_ge(qk_added, 4 * i + c + 1)
                dve.tensor_tensor(qk[:, c, :].rearrange("p (h d) -> p h d", d=DHEAD),
                                  straight[:, c, :].rearrange("p (h d) -> p h d", d=DHEAD),
                                  spread(rnorm[:, 8 * c:8 * c + 8], [P, 8, DHEAD]), ALU.mult).then_inc(k_normed, 1)

            def previous_keys(n, s):
                dve.wait_ge(tr_evac, job(n, of_tile_before(s, "KT1")) + 1)
                keep = 1.0 if s == 1 else inside[:, bass.ds(n % (TPB // 2), 1)]
                dve.tensor_scalar(kT[:, s, :, :, 0:WINDOW].rearrange("p j h t -> p (j h) t"),
                                  kT[:, 1 - s, :, :, P:P + WINDOW].rearrange("p j h t -> p (j h) t"), keep, None, ALU.mult).then_inc(kprev_done, 1)

            def begin_residual(n):
                c = pair_column(n - 1)
                dve.wait_ge(wo_begun, n)
                dve.tensor_tensor(x1T[:, bass.ds(c, 2 * P)], psum[:, 2, 0:2 * P], xT[:, bass.ds(c, 2 * P)], ALU.add).then_inc(x1_begun, 1)

            def attention_residual(n):
                c = pair_column(n - 1)
                dve.wait_ge(x1_begun, n)
                dve.wait_ge(tr_evac, job(n, "A*WO") + 1)
                dve.tensor_tensor(x1T[:, bass.ds(c, 2 * P)], y1[:], x1T[:, bass.ds(c, 2 * P)], ALU.add).then_inc(x1_done, 1)

            def shift_pair(n):
                c = pair_column(n - 1)
                dve.wait_ge(x1_done, n)
                dve.tensor_scalar(xs2[0:64, :], x1T[0:64, bass.ds(c, 2 * P)], 1.0, None, ALU.mult)
                dve.tensor_scalar(xs2[64:P, :], x1T[64:P, bass.ds(c - 1, 2 * P)], 1.0, None, ALU.mult).then_inc(xs2_done, 1)

            def layernorm_mean(n):
                dve.wait_ge(tr_evac, job(n, "B*XT") + 1)
                dve.tensor_scalar(nmean[:], lmean[:], -1.0 / DIM, None, ALU.mult).then_inc(ln_done, 1)

            def layernorm_variance(n):
                dve.wait_ge(ln_squared, n)
                dve.tensor_scalar(lvare[:], lvar[:], 1.0 / DIM, 1e-5, ALU.mult, ALU.add).then_inc(ln_done, 1)

            def layernorm_rsqrt(n):
                dve.wait_ge(ln_done, 2 * n)
                return Rsqrt(dve, ln_newton, STEPS * (n - 1), lvare[:], lvarc[:], rstd[:], la[:], lb[:])

            def layernorm_apply(n):
                dve.wait_ge(ln_newton, STEPS * n)
                for t in range(2):
                    last = dve.tensor_scalar(xn_tok[:, t, :], x_tok[:, t, :], nmean[:, t:t + 1], rstd[:, t:t + 1], ALU.add, ALU.mult)
                last.then_inc(xn_done, 1)

            def gated(n, j):
                m = FFB[j]
                dve.wait_ge(tr_evac, job(n, f"B*H{j}") + 1)
                dve.tensor_tensor(hidden[0:m, j, :], up[0:m, j, :], gate[0:m, j, :], ALU.mult).then_inc(hidden_done, 1)

            def ffn_residual(n):
                c = pair_column(n - 1)
                dve.wait_ge(tr_evac, job(n, "B*FO") + 1)
                dve.tensor_tensor(xT[:, bass.ds(c, 2 * P)], y2[:], x1T[:, bass.ds(c, 2 * P)], ALU.add).then_inc(x2_done, 1)

            def turn(n):
                new, old = has_pair(n), has_before(n)
                i = 2 * n
                if old:
                    invert_sum(i - 1, 1)
                if new:
                    rotate(i, 0, 0)
                    rotate(i, 0, 1)
                if old:
                    top_of(i - 1, 2)
                if new:
                    roots = norms(i, 0)
                    roots.steps(6)
                if old:
                    top_of(i - 1, 3)
                    invert_sum(i - 1, 2)
                if new:
                    roots.steps(5)
                    scale_k(i, 0)
                if old:
                    invert_sum(i - 1, 3)
                    begin_residual(n)
                if new and old:
                    previous_keys(n, 0)
                if new:
                    rotate(i, 0, 2)
                    rotate(i, 0, 3)
                    roots = norms(i, 1)
                    roots.steps(4)
                    top_of(i, 0)
                    roots.steps(3)
                    top_of(i, 1)
                    roots.steps(2)
                    shift(n, 1)
                    roots.steps(2)
                    scale_k(i, 1)
                    invert_sum(i, 0)
                i = 2 * n + 1
                if old:
                    attention_residual(n)
                if new:
                    invert_sum(i - 1, 1)
                if old:
                    shift_pair(n)
                if new:
                    rotate(i, 1, 0)
                if old:
                    layernorm_mean(n)
                if new:
                    rotate(i, 1, 1)
                    roots = norms(i, 0)
                    roots.steps(1)
                if old:
                    layernorm_variance(n)
                    root = layernorm_rsqrt(n)
                    root.steps(1)
                if new:
                    roots.steps(1)
                if old:
                    root.steps(1)
                if new:
                    top_of(i - 1, 2)
                if old:
                    root.steps(1)
                if new:
                    roots.steps(2)
                if old:
                    root.steps(1)
                if new:
                    roots.steps(2)
                if old:
                    root.steps(3)
                if new:
                    roots.steps(1)
                if old:
                    root.steps(2)
                if new:
                    top_of(i - 1, 3)
                    roots.steps(2)
                if old:
                    root.steps(1)
                if new:
                    invert_sum(i - 1, 2)
                    roots.steps(1)
                if old:
                    root.steps(1)
                if new:
                    roots.steps(1)
                if old:
                    layernorm_apply(n)
                if new:
                    previous_keys(n, 1)
                    scale_k(i, 0)
                    rotate(i, 1, 2)
                    invert_sum(i - 1, 3)
                if new and has_next(n):
                    shift(n + 1, 0)
                if new:
                    rotate(i, 1, 3)
                    roots = norms(i, 1)
                    roots.steps(1)
                if old:
                    gated(n, 0)
                if new:
                    roots.steps(4)
                    top_of(i, 0)
                    roots.steps(2)
                if old:
                    gated(n, 1)
                if new:
                    roots.steps(4)
                if old:
                    gated(n, 2)
                if new:
                    top_of(i, 1)
                if old:
                    ffn_residual(n)
                if new:
                    invert_sum(i, 0)
                    scale_k(i, 1)

            dve.memset(kT[:], 0.0).then_inc(zeroed, 1)
            dve.memset(v_tok[:], 0.0).then_inc(zeroed, 1)
            dve.memset(norm2[:], 1.0).then_inc(zeroed, 1)
            dve.memset(x1T[:], 0.0).then_inc(zeroed, 1)
            dve.wait_ge(zeroed, 4)
            shift(0, 0)
            over_turns(dve, turn)

        @block.gpsimd
        def _(pool):
            def fold(i, n, s):
                pool.wait_ge(scales_loaded, i // TILES * 16 + 16)
                wait(pool, norm2_done, 4 * (i - 1))
                at = (n % (TPB // 2) * 2 + s) * (4 * DHEAD)
                pool.tensor_tensor(turn_tables[:, s, :], tables[:, bass.ds(at, 4 * DHEAD)], qk_scales[:], ALU.mult).then_inc(tables_done, 1)

            def normalise(i, q):
                pool.wait_ge(rec_done, 4 * i + q + 1)
                pool.tensor_tensor(heads4(probs_n[:, q, :]), heads4(probs[:, q, :]),
                                   spread(rtotal[:, 4 * q:4 * q + 4], [P, 4, KEYS]), ALU.mult).then_inc(probs_normed, 1)

            def add(i, c):
                pool.wait_ge(rotary_done, 4 * i + c + 1)
                pool.tensor_tensor(straight[:, c, :], straight[:, c, :], crossed[:, c, :], ALU.add).then_inc(qk_added, 1)

            def scale_q(i, half):
                c = 2 * half
                pool.wait_ge(newton, STEPS * (2 * i + half + 1))
                pool.wait_ge(qk_added, 4 * i + c + 1)
                pool.tensor_tensor(qk[:, c, :].rearrange("p (h d) -> p h d", d=DHEAD),
                                   straight[:, c, :].rearrange("p (h d) -> p h d", d=DHEAD),
                                   spread(rnorm[:, 8 * c:8 * c + 8], [P, 8, DHEAD]), ALU.mult).then_inc(q_normed, 1)

            def turn(n):
                new, old = has_pair(n), has_before(n)
                i = 2 * n
                if old:
                    normalise(i - 1, 1)
                if new:
                    add(i, 0)
                    add(i, 1)
                if old:
                    normalise(i - 1, 2)
                if new:
                    scale_q(i, 0)
                if old:
                    normalise(i - 1, 3)
                if new:
                    add(i, 2)
                    fold(i + 1, n, 1)
                    add(i, 3)
                    scale_q(i, 1)
                    normalise(i, 0)
                i = 2 * n + 1
                if new:
                    normalise(i - 1, 1)
                    add(i, 0)
                    add(i, 1)
                    normalise(i - 1, 2)
                    scale_q(i, 0)
                if new and has_next(n):
                    fold(i + 1, n + 1, 0)
                if new:
                    normalise(i - 1, 3)
                    add(i, 2)
                    scale_q(i, 1)
                    add(i, 3)
                    normalise(i, 0)

            fold(0, 0, 0)
            over_turns(pool, turn)


def window_attention(nc, dram, const, base, xT, psum):
    ident, ident16, masks = const["ident"], const["ident16"], const["masks"]
    HD = DIM // HEADS
    BLOCKS = 2 * TILES
    ctx = ExitStack()
    with ctx:
        def sb(n, shape, dt=FP32):
            return ctx.enter_context(nc.sbuf_tensor(f"wa_{n}", shape, dt))

        def sem(n):
            return ctx.enter_context(nc.semaphore(f"wa_{n}"))

        w = sb("w", [P, 4, DIM])
        head_rows = sb("head_rows", [P, HEADS])
        qTall = sb("qTall", [P, TILES * P])
        kTall = sb("kTall", [P, BATCH * PADDED])
        v_win = sb("v_win", [KEYS, BLOCKS, DIM])
        q_heads = sb("q_heads", [P, 2, HEADS, P])
        k_tile = sb("k_tile", [P, 2, WINDOW + P])
        v_tile = sb("v_tile", [KEYS, 2, 2, DIM])
        neg_top = sb("neg_top", [P, HEADS])
        probs = sb("probs", [P, 4, QUAD])
        total, rtotal = sb("total", [P, HEADS]), sb("rtotal", [P, HEADS])
        probs_n = sb("probs_n", [P, 4, QUAD])
        pT = sb("pT", [KEYS, 4, 4 * P])
        o_tok = sb("o_tok", [P, DIM])
        oT = sb("oT", [P, P])

        loaded, kv_full, kv_evac, q_spread = sem("loaded"), sem("kv_full"), sem("kv_evac"), sem("q_spread")
        s_full, max_done, exp_done = sem("s_full"), sem("max_done"), sem("exp_done")
        rec_done, probs_normed = sem("rec_done"), sem("probs_normed")
        p_turned, p_evac, o_full, o_evac = sem("p_turned"), sem("p_evac"), sem("o_full"), sem("o_evac")
        o_turned, oT_evac, y_full, y_added = sem("o_turned"), sem("oT_evac"), sem("y_full"), sem("y_added")
        k_zeroed = sem("k_zeroed")
        block = ctx.enter_context(nc.Block())

        def s_bank(q):
            return psum[:, q % 2, 0:QUAD]

        GROUPS = 2 * (TILES // 4) + BLOCKS // 4

        @block.sync
        def _(sp):
            sp.dma_start(w[:], dram["Wattn"].rearrange("f p n -> p f n")).then_inc(loaded, 16)
            sp.dma_start(head_rows[:], dram["head_rows"]).then_inc(loaded, 16)

        @block.tensor
        def _(pe):
            pe.wait_ge(loaded, 32)
            for g in range(GROUPS):
                if g >= 8:
                    pe.wait_ge(kv_evac, g - 7)
                if g < 8:
                    c = pair_column(2 * (g % 4))
                    nc.tensor.matmul(psum[:, g % 8, :], w[:, g // 4, :], xT[:, c:c + 4 * P], start=True, stop=True).then_inc(kv_full, 1)
                else:
                    for j in range(4):
                        b = 4 * (g - 8) + j
                        c = pair_column(b // 4) + b % 4 * 64 - WINDOW
                        last = nc.tensor.matmul(psum[0:KEYS, g % 8, j * P:(j + 1) * P], xT[:, c:c + KEYS], w[:, 2, :],
                                                start=True, stop=True, skip_group_check=True)
                    last.then_inc(kv_full, 1)
            pe.wait_ge(kv_evac, GROUPS)

            def scores(t, s, q):
                wait(pe, exp_done, 4 * t + q - 1)
                pe.wait_ge(q_spread, t + 1)
                mask = masks[:, bass.ds(t // 2 % (TPB // 2) * QUAD, QUAD)] if s == 0 else masks[:, QUAD:2 * QUAD]
                nc.tensor.matmul(s_bank(q), ident16[:], mask, start=True, stop=False, skip_group_check=True)
                for h in range(4):
                    for b in range(2):
                        last = nc.tensor.matmul(s_bank(q)[64 * b:64 * b + 64, h * KEYS:(h + 1) * KEYS],
                                                q_heads[:, s, 4 * q + h, 64 * b:64 * b + 64],
                                                k_tile[:, s, 64 * b:64 * b + KEYS], start=False, stop=True, skip_group_check=True)
                last.then_inc(s_full, 1)

            def turn_probs(t, q):
                wait(pe, p_evac, 4 * t + q - 1)
                pe.wait_ge(probs_normed, 4 * t + q + 1)
                for h in range(4):
                    last = nc.tensor.transpose(psum[0:KEYS, 2 + q % 2, h * P:(h + 1) * P], probs_n[:, q, h * KEYS:(h + 1) * KEYS], ident[:])
                last.then_inc(p_turned, 1)

            def tile(t, s):
                scores(t, s, 0)
                scores(t, s, 1)
                scores(t, s, 2)
                turn_probs(t, 0)
                scores(t, s, 3)
                for q in range(1, 4):
                    turn_probs(t, q)
                wait(pe, o_evac, t)
                pe.wait_ge(p_evac, 4 * t + 4)
                for h in range(HEADS):
                    for b in range(2):
                        last = nc.tensor.matmul(psum[64 * b:64 * b + 64, 4, h * HD:(h + 1) * HD],
                                                pT[:, h // 4, h % 4 * P + 64 * b:h % 4 * P + 64 * b + 64],
                                                v_tile[:, s, b, h * HD:(h + 1) * HD],
                                                start=True, stop=True, skip_group_check=True)
                last.then_inc(o_full, 1)
                pe.wait_ge(o_evac, t + 1)
                wait(pe, oT_evac, t)
                nc.tensor.transpose(psum[:, 5, 0:P], o_tok[:], ident[:]).then_inc(o_turned, 1)
                pe.wait_ge(oT_evac, t + 1)
                wait(pe, y_added, t)
                nc.tensor.matmul(psum[:, 6, 0:DIM], oT[:], w[:, 3, :], start=True, stop=True).then_inc(y_full, 1)

            tile(0, 0)
            tile(1, 1)
            with pe.Fori(1, TILES // 2) as p:
                tile(2 * p, 0)
                tile(2 * p + 1, 1)

        @block.scalar
        def _(act):
            act.wait_ge(k_zeroed, 1)
            for g in range(GROUPS):
                act.wait_ge(kv_full, g + 1)
                if g < 4:
                    nc.scalar.activation(qTall[:, 4 * P * g:4 * P * (g + 1)], psum[:, g, :], ACT.Copy, scale=1.0 / float(np.sqrt(HD))).then_inc(kv_evac, 1)
                elif g < 8:
                    c = pair_column(2 * (g - 4))
                    nc.scalar.activation(kTall[:, c:c + 4 * P], psum[:, g, :], ACT.Copy).then_inc(kv_evac, 1)
                else:
                    nc.scalar.activation(v_win[:, 4 * (g - 8):4 * (g - 7), :], psum[0:KEYS, g % 8, :].rearrange("p (j d) -> p j d", j=4), ACT.Copy).then_inc(kv_evac, 1)

            def exps(t, q):
                act.wait_ge(max_done, 4 * t + q + 1)
                wait(act, probs_normed, 4 * (t - 1) + q + 1)
                for h in range(4):
                    at, one = slice(h * KEYS, (h + 1) * KEYS), slice(4 * q + h, 4 * q + h + 1)
                    last = nc.scalar.activation(probs[:, q, at], s_bank(q)[:, at], ACT.Exp, bias=neg_top[:, one], accum_out=total[:, one])
                last.then_inc(exp_done, 1)

            def evac_p(t, q):
                act.wait_ge(p_turned, 4 * t + q + 1)
                nc.scalar.activation(pT[:, q, :], psum[0:KEYS, 2 + q % 2, :], ACT.Copy).then_inc(p_evac, 1)

            def tile(t):
                exps(t, 0)
                exps(t, 1)
                exps(t, 2)
                wait(act, o_full, t)
                evac_p(t, 0)
                exps(t, 3)
                for q in range(1, 4):
                    evac_p(t, q)
                act.wait_ge(o_full, t + 1)
                nc.scalar.activation(o_tok[:], psum[:, 4, 0:P], ACT.Copy).then_inc(o_evac, 1)
                act.wait_ge(o_turned, t + 1)
                nc.scalar.activation(oT[:], psum[:, 5, 0:P], ACT.Copy).then_inc(oT_evac, 1)

            tile(0)
            with act.Fori(1, TILES) as t:
                tile(t)

        @block.vector
        def _(dve):
            dve.memset(kTall[:], 0.0).then_inc(k_zeroed, 1)

            def top_of(t, q):
                dve.wait_ge(s_full, 4 * t + q + 1)
                dve.tensor_reduce(neg_top[:, 4 * q:4 * q + 4], heads4(s_bank(q)), AX_X, ALU.max, negate=True).then_inc(max_done, 1)

            def invert_sum(t, q):
                dve.wait_ge(exp_done, 4 * t + q + 1)
                wait(dve, probs_normed, 4 * (t - 1) + q + 1)
                dve.reciprocal(rtotal[:, 4 * q:4 * q + 4], total[:, 4 * q:4 * q + 4]).then_inc(rec_done, 1)

            def tile(t):
                top_of(t, 0)
                top_of(t, 1)
                invert_sum(t, 0)
                top_of(t, 2)
                invert_sum(t, 1)
                top_of(t, 3)
                invert_sum(t, 2)
                invert_sum(t, 3)
                dve.wait_ge(y_full, t + 1)
                row = base[:, bass.ds(t, 1), :].rearrange("p o d -> p (o d)")
                dve.tensor_tensor(row, psum[:, 6, 0:DIM], row, ALU.add).then_inc(y_added, 1)

            tile(0)
            with dve.Fori(1, TILES) as t:
                tile(t)

        @block.gpsimd
        def _(pool):
            def q_by_head(t, s):
                pool.wait_ge(kv_evac, GROUPS)
                wait(pool, o_full, t - 1)
                pool.tensor_copy(k_tile[:, s, :], kTall[:, bass.ds(pair_column(t // 2) + s * P - WINDOW, WINDOW + P)])
                pool.tensor_copy(v_tile[:, s, :, :], v_win[:, bass.ds(2 * t, 2), :])
                q_t = qTall[:, bass.ds(t * P, P)]
                pool.tensor_tensor(q_heads[:, s, :, :], q_t.unsqueeze(1).broadcast_to([P, HEADS, P]),
                                   spread(head_rows[:], [P, HEADS, P]), ALU.mult).then_inc(q_spread, 1)

            def normalise(t, q):
                pool.wait_ge(rec_done, 4 * t + q + 1)
                wait(pool, p_turned, 4 * (t - 1) + q + 1)
                pool.tensor_tensor(heads4(probs_n[:, q, :]), heads4(probs[:, q, :]),
                                   spread(rtotal[:, 4 * q:4 * q + 4], [P, 4, KEYS]), ALU.mult).then_inc(probs_normed, 1)

            pool.wait_ge(loaded, 32)
            q_by_head(0, 0)
            q_by_head(1, 1)
            for q in range(4):
                normalise(0, q)
            with pool.Fori(1, TILES // 2) as p:
                q_by_head(2 * p, 0)
                for q in range(4):
                    normalise(2 * p - 1, q)
                q_by_head(2 * p + 1, 1)
                for q in range(4):
                    normalise(2 * p, q)
            for q in range(4):
                normalise(TILES - 1, q)


def macaron(nc, dram, out):
    ctx = ExitStack()
    with ctx:
        def sb(n, shape, dt=FP32):
            return ctx.enter_context(nc.sbuf_tensor(n, shape, dt))

        base = sb("base", [P, TILES, DIM])
        xT = sb("xT", [P, BATCH * PADDED])
        const = {
            "ident": sb("ident", [P, P]), "ident16": sb("ident16", [P, P], BF16),
            "masks": sb("masks", [P, TPB // 2 * QUAD], BF16), "tables": sb("tables", [P, TPB * 4 * DHEAD]),
            "inside": sb("inside", [P, TPB // 2]),
        }
        psum = ctx.enter_context(nc.psum_tensor("psum", [P, 8, 512], FP32))

        with ExitStack() as load:
            arrived = load.enter_context(nc.semaphore("arrived"))
            cleared = load.enter_context(nc.semaphore("cleared"))
            block = load.enter_context(nc.Block())

            @block.sync
            def _(sp):
                sp.dma_start(base[:], dram["x"].rearrange("t p d -> p t d")).then_inc(arrived, 16)
                for n, t in const.items():
                    sp.dma_start(t[:], dram[n]).then_inc(arrived, 16)
                sp.wait_ge(arrived, 16 * (1 + len(const)))

            @block.vector
            def _(dve):
                dve.memset(xT[:], 0.0).then_inc(cleared, 1)
                dve.wait_ge(cleared, 1)

        layernorm_to_columns(nc, base, xT, const["ident"], psum, "ln1")
        stack(nc, dram, const, xT, psum, "f1")
        add_half_of_columns(nc, base, xT, const["ident"], psum, "r1")
        layernorm_to_columns(nc, base, xT, const["ident"], psum, "ln2")
        window_attention(nc, dram, const, base, xT, psum)
        layernorm_to_columns(nc, base, xT, const["ident"], psum, "ln3")
        stack(nc, dram, const, xT, psum, "f2")
        add_half_of_columns(nc, base, xT, const["ident"], psum, "r2")

        with ExitStack() as store:
            stored = store.enter_context(nc.semaphore("stored"))
            block = store.enter_context(nc.Block())

            @block.sync
            def _(sp):
                sp.dma_start(out.rearrange("t p d -> p t d"), base[:]).then_inc(stored, 16)
                sp.wait_ge(stored, 16)


def rotary_constants():
    f = np.float32
    half = np.arange(0, DHEAD, 2, dtype=f)
    inv_freq = (f(1.0) / f(10000.0) ** (half / f(DHEAD))).astype(f)
    t = np.arange(SEQ, dtype=f)
    freqs = (t[:, None] * inv_freq[None, :]).astype(f)
    freqs = np.concatenate([freqs, freqs], -1)
    base_scale = (half + f(0.4 * DHEAD)) / f(1.4 * DHEAD)
    power = (t - SEQ // 2) / f(WINDOW // 2)
    scale = (base_scale[None, :].astype(f) ** power[:, None].astype(f)).astype(f)
    scale = np.concatenate([scale, scale], -1)
    sign = np.where(np.arange(DHEAD) < DHEAD // 2, f(-1), f(1))
    cos, sin = np.cos(freqs), np.sin(freqs) * sign
    inv = f(1.0) / scale
    table = np.stack([cos * scale, sin * scale, cos * inv, sin * inv], 1).astype(f)
    return np.ascontiguousarray(table.reshape(TPB, P, 4 * DHEAD).transpose(1, 0, 2).reshape(P, -1))


def mask_constants():
    q = np.arange(P)[:, None] % 64
    k = np.arange(KEYS)[None, :]
    plain = np.where((k >= q) & (k <= q + WINDOW), 0.0, MASKED)
    start = np.where((np.arange(P)[:, None] < 64) & (k < WINDOW), MASKED, plain)
    rows = [np.tile(start, (1, 4))] + [np.tile(plain, (1, 4))] * (TPB // 2 - 1)
    return np.concatenate(rows, 1)


def kernel(L0_attn_x, L0_attn_Wq, L0_attn_Wk, L0_attn_Wv, L0_attn_Wo, L0_ffn_Wqkv, L0_ffn_q_scale,
           L0_ffn_k_scale, L0_ffn_Wo, L0_ffn_ln_g, L0_ffn_ln_b, L0_ffn_W1, L0_ffn_b1, L0_ffn_W2, L0_ffn_b2):
    import concourse.bacc as bacc
    import ml_dtypes
    from concourse.bass_utils import run_bass_kernel_spmd

    a = lambda x: np.ascontiguousarray(np.asarray(x))
    hd = DHEAD // 2
    qs, ks = a(L0_ffn_q_scale), a(L0_ffn_k_scale)
    swap = lambda s: np.concatenate([s[:, hd:], s[:, :hd]], 1)
    scales = np.concatenate([qs, swap(qs), ks, swap(ks)], 1)
    b1 = a(L0_ffn_b1)
    cols = np.zeros((DEPTH, P, 9), np.float32)
    cols[:, :, 0], cols[:, :, 1], cols[:, :, 8] = a(L0_ffn_ln_g), a(L0_ffn_ln_b), a(L0_ffn_b2)
    for part in range(2):
        for j, m in enumerate(FFB):
            cols[:, :m, 2 + 3 * part + j] = b1[:, part * FF + j * P:part * FF + j * P + m]
    arrays = {
        "x": a(L0_attn_x).reshape(TILES, P, DIM),
        "Wattn": np.stack([a(w).T for w in (L0_attn_Wq, L0_attn_Wk, L0_attn_Wv, L0_attn_Wo)]),
        "Wqkv": a(L0_ffn_Wqkv), "Wo": a(L0_ffn_Wo), "W1": a(L0_ffn_W1), "W2": a(L0_ffn_W2),
        "qk_scales": np.ascontiguousarray(np.broadcast_to(scales[:, None, :], (DEPTH, P, 4 * DHEAD))),
        "ffn_cols": cols,
        "ident": np.eye(P, dtype=np.float32), "ident16": np.eye(P).astype(ml_dtypes.bfloat16),
        "masks": mask_constants().astype(ml_dtypes.bfloat16), "tables": rotary_constants(),
        "inside": np.tile(np.arange(TPB // 2) > 0, (P, 1)).astype(np.float32),
        "head_rows": (np.arange(P)[:, None] // (DIM // HEADS) == np.arange(HEADS)[None, :]).astype(np.float32),
    }
    nc = bacc.Bacc("TRN2", target_bir_lowering=False, num_devices=1)
    dram = {n: nc.dram_tensor(f"in_{n}", v.shape, mybir.dt.from_np(v.dtype), kind="ExternalInput").ap() for n, v in arrays.items()}
    out = nc.dram_tensor("out", (TILES, P, DIM), FP32, kind="ExternalOutput").ap()
    macaron(nc, dram, out)
    r = run_bass_kernel_spmd(nc, [{f"in_{n}": v for n, v in arrays.items()}], core_ids=[0])
    return r.results[0]["out"].reshape(BATCH, SEQ, DIM)
```

```python
from contextlib import ExitStack

import numpy as np

import concourse.bass as bass
from concourse import mybir

FP32 = mybir.dt.float32
BF16 = mybir.dt.bfloat16
INT32 = mybir.dt.int32
ALU = mybir.AluOpType
ACT = mybir.ActivationFunctionType
AX_X = mybir.AxisListType.X

P = 128
BATCH, SEQ, DIM = 2, 1024, 128
DEPTH, HEADS, DHEAD = 6, 16, 64
WINDOW = 32
INNER = HEADS * DHEAD
FF = int(DIM * 4 * 2 / 3)
FFB = [P, P, FF - 2 * P]
TILES = BATCH * SEQ // P
PAIRS = TILES // 2
TPB = SEQ // P
PADDED = WINDOW + SEQ
KEYS = 64 + WINDOW
QUAD = 4 * KEYS
BODIES = DEPTH * PAIRS
MASKED = -1.0e30
RSQRT_MAGIC = float(0x5F3759DF)
STEPS = 11
CHUNKS = ["q0", "k0", "v0", "q1", "k1", "v1"]
TURN_A = ["*QT1", "*KT1", "*PT0", "*PT1", "*OT0", "QT0", "KT0", "*PT2", "*PT3", "*OT1", "*WO"]
TURN_B = ["QT1", "*XT", "KT1", "PT0", "PT1", "OT0", "PT2", "QT0", "*XN", "PT3", "KT0", "*H0", "*H1", "*H2",
          "OT1", "*FO"]
TURN = ["A" + x for x in TURN_A] + ["B" + x for x in TURN_B]
FIRST_TURN = [x for x in TURN if "*" not in x]
REST = [x for x in TURN if "*" in x]
SKIPPED = len(TURN) - len(FIRST_TURN)


def job(n, name):
    if isinstance(n, int) and n == 0:
        return FIRST_TURN.index(name)
    if isinstance(n, int) and n == BODIES:
        return len(TURN) * BODIES - SKIPPED + REST.index(name)
    return n * len(TURN) + (TURN.index(name) - SKIPPED)


def bank_of(n, name):
    if isinstance(n, int):
        return 5 + job(n, name) % 3
    return 5 + (TURN.index(name) - SKIPPED) % 3


assert len(TURN) % 3 == 0


def of_tile_before(s, name):
    return "B" + name if s else "A*" + name


def wait(eng, sem, value):
    if not (isinstance(value, int) and value <= 0):
        eng.wait_ge(sem, value)


def known(eng, value):
    return value if isinstance(value, int) else eng.snap(value)


def pair_column(n):
    p = n % PAIRS
    return p * (2 * P) + p // (PAIRS // 2) * WINDOW + WINDOW


def over_turns(eng, body):
    body(0)
    with eng.Fori(1, BODIES - 1) as n:
        body(n)
    body(BODIES - 1)
    body(BODIES)


def has_pair(n):
    return not (isinstance(n, int) and n == BODIES)


def has_before(n):
    return not (isinstance(n, int) and n == 0)


def has_next(n):
    return not (isinstance(n, int) and n >= BODIES - 1)


def heads4(ap):
    return ap.rearrange("p (h k) -> p h k", h=4)


def spread(ap, shape):
    return ap.unsqueeze(2).broadcast_to(shape)


class Rsqrt:

    def __init__(self, eng, done, count, x, xc, y, a, b):
        self.eng, self.done, self.count = eng, done, count
        self.x, self.xc, self.y, self.a, self.b = x, xc, y, a, b
        self.k = 0

    def step(self):
        e, k = self.eng, self.k
        if k:
            e.wait_ge(self.done, self.count + k)
        if k == 0:
            i = e.tensor_scalar(self.xc, self.x, 1e-24, None, ALU.max)
        elif k == 1:
            i = e.tensor_scalar(self.y.bitcast(INT32), self.xc.bitcast(INT32), -0.5, RSQRT_MAGIC, ALU.mult, ALU.add)
        elif k % 3 == 2:
            i = e.scalar_tensor_tensor(self.a, self.y, -0.5, self.y, ALU.mult, ALU.mult)
        elif k % 3 == 0:
            i = e.tensor_tensor(self.b, self.a, self.xc, ALU.mult)
        else:
            i = e.scalar_tensor_tensor(self.y, self.b, 1.5, self.y, ALU.add, ALU.mult)
        i.then_inc(self.done, 1)
        self.k += 1

    def steps(self, count):
        for _ in range(count):
            self.step()


def layernorm_to_columns(nc, base, xT, ident, psum, name, scratch=None, sync=None, gpsimd=None):
    with ExitStack() as ctx:
        sb = lambda n, s: ctx.enter_context(nc.sbuf_tensor(f"{name}_{n}", s, FP32))
        sem = lambda n: ctx.enter_context(nc.semaphore(f"{name}_{n}"))
        centred, square = scratch or (sb("centred", [P, TILES, DIM])[:], sb("square", [P, TILES, DIM])[:])
        GROUPS = [slice(4 * g, 4 * g + 4) for g in range(TILES // 4)]
        mean, var, varc = sb("mean", [P, TILES]), sb("var", [P, TILES]), sb("varc", [P, TILES])
        rstd, ta, tb = sb("rstd", [P, TILES]), sb("ta", [P, TILES]), sb("tb", [P, TILES])
        stats, newton, normed, turned, evacuated = (sem(x) for x in ("stats", "newton", "normed", "turned", "evacuated"))
        centred_done, squared = sem("centred_done"), sem("squared")
        block = ctx.enter_context(nc.Block())

        @block.vector
        def _(dve):
            full = [P, 4, DIM]
            dve.tensor_reduce(mean[:], base[:], AX_X, ALU.add).then_inc(stats, 1)
            dve.wait_ge(stats, 1)
            dve.tensor_scalar(mean[:], mean[:], -1.0 / DIM, None, ALU.mult).then_inc(stats, 1)
            dve.wait_ge(stats, 2)
            for g in GROUPS:
                dve.tensor_tensor(centred[:, g, :], base[:, g, :], spread(mean[:, g], full), ALU.add).then_inc(centred_done, 1)
            for k, g in enumerate(GROUPS):
                dve.wait_ge(squared, k + 1)
                dve.tensor_reduce(var[:, g], square[:, g, :], AX_X, ALU.add).then_inc(stats, 1)
            dve.wait_ge(stats, 6)
            dve.tensor_scalar(var[:], var[:], 1.0 / DIM, 1e-5, ALU.mult, ALU.add).then_inc(stats, 1)
            dve.wait_ge(stats, 7)
            Rsqrt(dve, newton, 0, var[:], varc[:], rstd[:], ta[:], tb[:]).steps(STEPS)
            dve.wait_ge(newton, STEPS)
            for g in GROUPS:
                dve.tensor_tensor(centred[:, g, :], centred[:, g, :], spread(rstd[:, g], full), ALU.mult).then_inc(normed, 1)

        @block.tensor
        def _(pe):
            for t in range(TILES):
                if t % 4 == 0:
                    pe.wait_ge(normed, t // 4 + 1)
                last = nc.tensor.transpose(psum[:, t // 4, t % 4 * P:(t % 4 + 1) * P], centred[:, t, :], ident[:])
                if t % 4 == 3:
                    last.then_inc(turned, 1)

        @block.scalar
        def _(act):
            for k, g in enumerate(GROUPS):
                act.wait_ge(centred_done, k + 1)
                nc.scalar.activation(square[:, g, :], centred[:, g, :], ACT.Square).then_inc(squared, 1)
            for g in range(TILES // 4):
                act.wait_ge(turned, g + 1)
                c = pair_column(2 * g)
                nc.scalar.activation(xT[:, c:c + 4 * P], psum[:, g, :], ACT.Copy).then_inc(evacuated, 1)

        if sync:
            block.sync(sync)
        if gpsimd:
            block.gpsimd(gpsimd)


def add_half_of_columns(nc, base, xT, ident, psum, name):
    with ExitStack() as ctx:
        sem = lambda n: ctx.enter_context(nc.semaphore(f"{name}_{n}"))
        turned, added = sem("turned"), sem("added")
        block = ctx.enter_context(nc.Block())

        @block.tensor
        def _(pe):
            for t in range(TILES):
                c = pair_column(t // 2) + t % 2 * P
                last = nc.tensor.transpose(psum[:, t // 4, t % 4 * P:(t % 4 + 1) * P], xT[:, c:c + P], ident[:])
                if t % 4 == 3:
                    last.then_inc(turned, 1)

        @block.vector
        def _(dve):
            for g in range(TILES // 4):
                dve.wait_ge(turned, g + 1)
                tiles = base[:, 4 * g:4 * g + 4, :].rearrange("p t d -> p (t d)")
                dve.scalar_tensor_tensor(tiles, psum[:, g, :], 0.5, tiles, ALU.mult, ALU.add).then_inc(added, 1)


def stack(nc, dram, const, base, xT, psum, name):
    ident, ident16, masks, tables = const["ident"], const["ident16"], const["masks"], const["tables"]
    inside = const["inside"]
    ctx = ExitStack()
    with ctx:
        def sb(n, shape, dt=FP32):
            return ctx.enter_context(nc.sbuf_tensor(f"{name}_{n}", shape, dt))

        def sem(n):
            return ctx.enter_context(nc.semaphore(f"{name}_{n}"))

        w_qkv = sb("w_qkv", [P, 3 * INNER])
        w_o = sb("w_o", [P, INNER // P, DIM])
        w_1 = sb("w_1", [P, 2 * FF])
        w_2 = sb("w_2", [P, 3, DIM])
        ffn_cols = sb("ffn_cols", [P, 9])
        qk_scales = sb("qk_scales", [P, 4 * DHEAD])
        x1T = sb("x1T", [P, BATCH * PADDED])
        xs = sb("xs", [P, 2, P])
        turn_tables = sb("turn_tables", [P, 2, 4 * DHEAD])
        squares = sb("squares", [P, 4, 512])
        norm2 = sb("norm2", [P, 2 * HEADS])
        norm2c = sb("norm2c", [P, 2 * HEADS])
        rnorm = sb("rnorm", [P, 2 * HEADS])
        na, nb = sb("na", [P, 2 * HEADS]), sb("nb", [P, 2 * HEADS])
        straight = sb("straight", [P, 4, 512])
        crossed = sb("crossed", [P, 4, 512])
        qk = sb("qk", [P, 4, 512])
        qT = sb("qT", [P, 8, P])
        kT = sb("kT", [P, 2, 8, 2, WINDOW + P])
        v_tok = sb("v_tok", [P, 2, INNER])
        v_win = sb("v_win", [KEYS, 2, 2, INNER])
        neg_top = sb("neg_top", [P, HEADS])
        probs = sb("probs", [P, 4, QUAD])
        total, rtotal = sb("total", [P, HEADS]), sb("rtotal", [P, HEADS])
        probs_n = sb("probs_n", [P, 4, QUAD])
        pT = sb("pT", [KEYS, 4, 4 * P])
        oT = sb("oT", [P, 8, 2 * P])
        y1 = sb("y1", [P, 2 * P])
        xs2 = sb("xs2", [P, 2 * P])
        x_tok = sb("x_tok", [P, 2, P])
        lmean, nmean, lvar, lvare, lvarc, rstd, la, lb = (sb(x, [P, 2]) for x in ("lmean", "nmean", "lvar", "lvare", "lvarc", "rstd", "la", "lb"))
        lsq = sb("lsq", [P, 2, P])
        xn_tok = sb("xn_tok", [P, 2, P])
        xnT = sb("xnT", [P, 2 * P])
        up = sb("up", [P, 3, 2 * P])
        gate = sb("gate", [P, 3, 2 * P])
        hidden = sb("hidden", [P, 3, 2 * P])
        y2 = sb("y2", [P, 2 * P])

        proj_full, s_full, tr_full, wo_begun = sem("proj_full"), sem("s_full"), sem("tr_full"), sem("wo_begun")
        tr_evac, v_evac, squared, exp_done = sem("tr_evac"), sem("v_evac"), sem("squared"), sem("exp_done")
        ln_squared = sem("ln_squared")
        xs_done, max_done, rec_done = (sem(x) for x in ("xs_done", "max_done", "rec_done"))
        rotary_done, norm2_done, newton, k_normed = sem("rotary_done"), sem("norm2_done"), sem("newton"), sem("k_normed")
        x1_begun = sem("x1_begun")
        kprev_done, x1_done, xs2_done, ln_done, xn_done = (sem(x) for x in ("kprev_done", "x1_done", "xs2_done", "ln_done", "xn_done"))
        hidden_done, x2_done, ln_newton = sem("hidden_done"), sem("x2_done"), sem("ln_newton")
        zeroed = sem("zeroed")
        tables_done, probs_normed, qk_added, q_normed = (sem(x) for x in ("tables_done", "probs_normed", "qk_added", "q_normed"))
        loaded = [sem("first_heads_loaded"), sem("last_heads_loaded")]
        scales_loaded, wo_loaded, ffn_loaded, v_moved = (sem(x) for x in ("scales_loaded", "wo_loaded", "ffn_loaded", "v_moved"))


        def s_bank(q):
            return psum[:, 3 + q % 2, 0:QUAD]

        def load_half(sp, l, half):
            if not (isinstance(l, int) and l == 0):
                sp.wait_ge(proj_full, known(sp, 6 * TILES * l - 3 + 3 * half))
            view = lambda ap: ap.rearrange("p (t h n) -> p t h n", t=3, h=2)[:, :, half, :]
            sp.dma_start(view(w_qkv[:]), view(dram["Wqkv"][bass.ds(l, 1), :, :].rearrange("o p n -> (o p) n"))).then_inc(loaded[half], 16)

        def load_scales(sp, l):
            wait(sp, tables_done, known(sp, TILES * l))
            sp.dma_start(qk_scales[:], dram["qk_scales"][bass.ds(l, 1), :, :].rearrange("o p n -> p (o n)")).then_inc(scales_loaded, 16)

        def load_wo(sp, l):
            if not (isinstance(l, int) and l == 0):
                wait(sp, tr_full, known(sp, job(PAIRS * l, "A*WO") + 1))
            sp.dma_start(w_o[:], dram["Wo"][bass.ds(l, 1), :, :].rearrange("o (j p) n -> p (o j) n", p=P)).then_inc(wo_loaded, 16)

        def load_ffn(sp, l):
            wait(sp, x2_done, known(sp, PAIRS * l))
            sp.dma_start(w_1[:], dram["W1"][bass.ds(l, 1), :, :].rearrange("o p n -> p (o n)")).then_inc(ffn_loaded, 16)
            sp.dma_start(w_2[:, 0:2, :], dram["W2"][bass.ds(l, 1), 0:2 * P, :].rearrange("o (j p) n -> p (o j) n", p=P)).then_inc(ffn_loaded, 16)
            sp.dma_start(w_2[0:FFB[2], 2, :], dram["W2"][bass.ds(l, 1), 2 * P:FF, :].rearrange("o p n -> p (o n)")).then_inc(ffn_loaded, 16)
            sp.dma_start(ffn_cols[:], dram["ffn_cols"][bass.ds(l, 1), :, :].rearrange("o p n -> p (o n)")).then_inc(ffn_loaded, 16)

        def load_first(sp):
            load_half(sp, 0, 0)
            load_scales(sp, 0)
            load_half(sp, 0, 1)
            load_wo(sp, 0)
            load_ffn(sp, 0)

        def clear(pool):
            x1_fronts = [x1T[:, b * PADDED:b * PADDED + WINDOW] for b in range(BATCH)]
            for k, zeros in enumerate([kT[:], v_tok[P - WINDOW:P, 1, :]] + x1_fronts):
                wait(pool, zeroed, k)
                pool.memset(zeros, 0.0).then_inc(zeroed, 1)

        tiles = lambda t: t[:].rearrange("p c (t d) -> p (c t) d", d=DIM)
        layernorm_to_columns(nc, base, xT, ident, psum, name + "_in", (tiles(straight), tiles(squares)), load_first, clear)
        block = ctx.enter_context(nc.Block())

        @block.sync
        def _(sp):
            def move_v(n, s):
                wait(sp, v_evac, 2 * (2 * n + s) + 2)
                now, before = v_tok[:, s, :], v_tok[:, 1 - s, :]
                sp.dma_start(v_win[0:WINDOW, s, 0, :], before[P - WINDOW:P, :]).then_inc(v_moved, 16)
                sp.dma_start(v_win[WINDOW:KEYS, s, 0, :], now[0:64, :]).then_inc(v_moved, 16)
                sp.dma_start(v_win[:, s, 1, :], now[WINDOW:P, :]).then_inc(v_moved, 16)

            def layer(l, first, last):
                n = PAIRS * l
                move_v(n, 0)
                if not first:
                    load_wo(sp, l)
                move_v(n, 1)
                if not first:
                    load_ffn(sp, l)
                with sp.Fori(1, PAIRS - 1) as p:
                    move_v(n + p, 0)
                    move_v(n + p, 1)
                move_v(n + PAIRS - 1, 0)
                if not last:
                    load_scales(sp, l + 1)
                    load_half(sp, l + 1, 0)
                    load_half(sp, l + 1, 1)
                move_v(n + PAIRS - 1, 1)

            layer(0, True, False)
            with sp.Fori(1, DEPTH - 1) as l:
                layer(l, False, False)
            layer(DEPTH - 1, False, True)

        @block.tensor
        def _(pe):
            def project(i, par, c):
                if c == 0:
                    pe.wait_ge(xs_done, i + 1)
                what, half = CHUNKS[c][0], int(CHUNKS[c][1])
                at = {"q": 0, "k": INNER, "v": 2 * INNER}[what] + 512 * half
                if c == 5 and par == 0 and not (isinstance(i, int) and i == 0):
                    pe.wait_ge(x1_begun, i // 2)
                elif what == "v":
                    wait(pe, v_evac, 2 * i + half)
                else:
                    wait(pe, norm2_done, 4 * i + 2 * half + c % 3 - 1)
                if what == "q":
                    pe.wait_ge(loaded[half], i // TILES * 16 + 16)
                nc.tensor.matmul(psum[:, c % 3, :], xs[:, par, :], w_qkv[:, at:at + 512],
                                 start=True, stop=True).then_inc(proj_full, 1)

            def scores(n, s, q):
                i, par = (2 * n + s, s) if q < 2 else (2 * n + s - 1, 1 - s)
                wait(pe, exp_done, 4 * i + q - 1)
                if q == 0:
                    pe.wait_ge(tr_evac, job(n, "AB"[s] + "KT0") + 1)
                    wait(pe, kprev_done, i)
                if q == 2:
                    pe.wait_ge(tr_evac, job(n, of_tile_before(s, "KT1")) + 1)
                mask = masks[:, bass.ds(n % (TPB // 2) * QUAD, QUAD)] if par == 0 else masks[:, QUAD:2 * QUAD]
                nc.tensor.matmul(s_bank(q), ident16[:], mask, start=True, stop=False, skip_group_check=True)
                for pr in range(2):
                    for b in range(2):
                        last = nc.tensor.matmul(
                            s_bank(q)[64 * b:64 * b + 64, pr * 2 * KEYS:(pr + 1) * 2 * KEYS],
                            qT[:, 2 * q + pr, 64 * b:64 * b + 64], kT[:, par, 2 * q + pr, :, 64 * b:64 * b + KEYS],
                            start=False, stop=True, skip_group_check=True)
                last.then_inc(s_full, 1)

            def tenant(n, name):
                wait(pe, tr_evac, job(n, name) - 2)
                return psum[:, bank_of(n, name), :]

            def turn_qk(n, s, what, half):
                name, i = ("AB"[s] + what + "0", 2 * n + s) if half == 0 else (of_tile_before(s, what + "1"), 2 * n + s - 1)
                bank = tenant(n, name)
                c = 2 * half + "QK".index(what[0])
                pe.wait_ge(q_normed if what[0] == "Q" else k_normed, 2 * i + half + 1)
                for j in range(4):
                    last = nc.tensor.transpose(bank[:, j * P:(j + 1) * P], qk[:, c, j * P:(j + 1) * P], ident[:])
                last.then_inc(tr_full, 1)

            def turn_probs(n, s, q):
                bank = tenant(n, of_tile_before(s, f"PT{q}"))
                pe.wait_ge(probs_normed, 4 * (2 * n + s - 1) + q + 1)
                for h in range(4):
                    last = nc.tensor.transpose(bank[0:KEYS, h * P:(h + 1) * P], probs_n[:, q, h * KEYS:(h + 1) * KEYS], ident[:])
                last.then_inc(tr_full, 1)

            def times_v(n, s, half):
                bank = tenant(n, of_tile_before(s, f"OT{half}"))
                pe.wait_ge(tr_evac, job(n, of_tile_before(s, f"PT{2 * half + 1}")) + 1)
                if half == 0:
                    pe.wait_ge(v_moved, 48 * (2 * n + s))
                for pr in range(4):
                    for b in range(2):
                        for h2 in range(2):
                            h = 8 * half + 2 * pr + h2
                            last = nc.tensor.matmul(
                                bank[64 * h2:64 * h2 + 64, pr * P + 64 * b:pr * P + 64 * b + 64],
                                v_win[:, 1 - s, b, h * DHEAD:(h + 1) * DHEAD],
                                pT[:, h // 4, h % 4 * P + 64 * b:h % 4 * P + 64 * b + 64],
                                start=True, stop=True, skip_group_check=True)
                last.then_inc(tr_full, 1)

            def times_wo(n, half):
                if half == 0:
                    pe.wait_ge(v_evac, 4 * BODIES if isinstance(n, int) and n == BODIES else 4 * n + 1)
                    pe.wait_ge(tr_evac, job(n, "A*OT0") + 1)
                    pe.wait_ge(wo_loaded, (n - 1) // PAIRS * 16 + 16)
                    bank = psum[:, 2, :]
                else:
                    bank = tenant(n, "A*WO")
                    pe.wait_ge(tr_evac, job(n, "A*OT1") + 1)
                for j in range(4 * half, 4 * half + 4):
                    last = nc.tensor.matmul(bank[:, 0:2 * P], w_o[:, j, :], oT[:, j, :], start=(j % 4 == 0), stop=(j % 4 == 3))
                last.then_inc(tr_full if half else wo_begun, 1)

            def ffn_tokens(n):
                bank = tenant(n, "B*XT")
                pe.wait_ge(xs2_done, n)
                for t in range(2):
                    last = nc.tensor.transpose(bank[:, t * P:(t + 1) * P], xs2[:, t * P:(t + 1) * P], ident[:])
                last.then_inc(tr_full, 1)

            def ffn_columns(n):
                bank = tenant(n, "B*XN")
                pe.wait_ge(xn_done, n)
                for t in range(2):
                    last = nc.tensor.transpose(bank[:, t * P:(t + 1) * P], xn_tok[:, t, :], ident[:])
                last.then_inc(tr_full, 1)

            def ffn_up(n, j):
                bank = tenant(n, f"B*H{j}")
                if j == 0:
                    pe.wait_ge(tr_evac, job(n, "B*XN") + 1)
                    pe.wait_ge(ffn_loaded, (n - 1) // PAIRS * 64 + 64)
                m = FFB[j]
                nc.tensor.matmul(bank[0:m, 0:2 * P], w_1[:, j * P:j * P + m], xnT[:], start=True, stop=True, skip_group_check=True)
                nc.tensor.matmul(bank[0:m, 2 * P:4 * P], w_1[:, FF + j * P:FF + j * P + m], xnT[:],
                                 start=True, stop=True, skip_group_check=True).then_inc(tr_full, 1)

            def ffn_down(n):
                bank = tenant(n, "B*FO")
                pe.wait_ge(hidden_done, 3 * n)
                for j, m in enumerate(FFB):
                    last = nc.tensor.matmul(bank[:, 0:2 * P], w_2[0:m, j, :], hidden[0:m, j, :], start=(j == 0), stop=(j == 2))
                last.then_inc(tr_full, 1)

            def turn(n):
                new, old = has_pair(n), has_before(n)
                i = 2 * n
                if new:
                    project(i, 0, 0)
                    project(i, 0, 1)
                if old:
                    turn_qk(n, 0, "QT", 1)
                    turn_qk(n, 0, "KT", 1)
                    turn_probs(n, 0, 0)
                if new:
                    project(i, 0, 2)
                if old:
                    turn_probs(n, 0, 1)
                    scores(n, 0, 2)
                    scores(n, 0, 3)
                    times_v(n, 0, 0)
                if new:
                    project(i, 0, 3)
                if old:
                    times_wo(n, 0)
                if new:
                    project(i, 0, 4)
                    turn_qk(n, 0, "QT", 0)
                    turn_qk(n, 0, "KT", 0)
                    project(i, 0, 5)
                if old:
                    turn_probs(n, 0, 2)
                    turn_probs(n, 0, 3)
                if new:
                    scores(n, 0, 0)
                if old:
                    times_v(n, 0, 1)
                if new:
                    scores(n, 0, 1)
                if old:
                    times_wo(n, 1)
                i = 2 * n + 1
                if new:
                    project(i, 1, 0)
                    project(i, 1, 1)
                    turn_qk(n, 1, "QT", 1)
                if old:
                    ffn_tokens(n)
                if new:
                    turn_qk(n, 1, "KT", 1)
                    project(i, 1, 2)
                    turn_probs(n, 1, 0)
                    turn_probs(n, 1, 1)
                    scores(n, 1, 2)
                    scores(n, 1, 3)
                    project(i, 1, 3)
                    times_v(n, 1, 0)
                    project(i, 1, 4)
                    project(i, 1, 5)
                    turn_probs(n, 1, 2)
                    turn_qk(n, 1, "QT", 0)
                if old:
                    ffn_columns(n)
                if new:
                    turn_probs(n, 1, 3)
                    turn_qk(n, 1, "KT", 0)
                if old:
                    ffn_up(n, 0)
                    ffn_up(n, 1)
                    ffn_up(n, 2)
                if new:
                    scores(n, 1, 0)
                    times_v(n, 1, 1)
                    scores(n, 1, 1)
                if old:
                    ffn_down(n)

            over_turns(pe, turn)

        @block.scalar
        def _(act):
            def evac(n, name):
                act.wait_ge(tr_full, job(n, name) + 1)
                return psum[:, bank_of(n, name), :]

            def evac_q(n, s, half):
                bank = evac(n, "AB"[s] + "QT0" if half == 0 else of_tile_before(s, "QT1"))
                wait(act, s_full, 4 * (2 * n + s - 1 - half) + 2 * half + 2)
                nc.scalar.activation(qT[:, 4 * half:4 * half + 4, :], bank.rearrange("p (j t) -> p j t", j=4),
                                     ACT.Copy, scale=8.0).then_inc(tr_evac, 1)

            def evac_k(n, s, half):
                bank, par = (evac(n, "AB"[s] + "KT0"), s) if half == 0 else (evac(n, of_tile_before(s, "KT1")), 1 - s)
                bank = bank.rearrange("p (j t) -> p j t", j=4)
                for h2 in range(2):
                    r = slice(64 * h2, 64 * h2 + 64)
                    last = nc.scalar.activation(kT[r, par, 4 * half:4 * half + 4, h2, WINDOW:], bank[r], ACT.Copy)
                last.then_inc(tr_evac, 1)

            def evac_v(i, par, half):
                act.wait_ge(proj_full, 6 * i + 3 * half + 3)
                wait(act, v_moved, 48 * i)
                nc.scalar.activation(v_tok[:, par, 512 * half:512 * half + 512], psum[:, 2, :], ACT.Copy).then_inc(v_evac, 1)

            def square(i, c):
                act.wait_ge(proj_full, 6 * i + c + c // 2 + 1)
                wait(act, norm2_done, 4 * (i - 1) + c + 1)
                nc.scalar.activation(squares[:, c, :], psum[:, c % 2, :], ACT.Square).then_inc(squared, 1)

            def exps(i, q):
                act.wait_ge(max_done, 4 * i + q + 1)
                wait(act, probs_normed, 4 * (i - 1) + q + 1)
                for h in range(4):
                    at, one = slice(h * KEYS, (h + 1) * KEYS), slice(4 * q + h, 4 * q + h + 1)
                    last = nc.scalar.activation(probs[:, q, at], s_bank(q)[:, at], ACT.Exp, bias=neg_top[:, one], accum_out=total[:, one])
                last.then_inc(exp_done, 1)

            def evac_p(n, s, q):
                bank = evac(n, of_tile_before(s, f"PT{q}"))
                nc.scalar.activation(pT[:, q, :], bank[0:KEYS, :], ACT.Copy).then_inc(tr_evac, 1)

            def evac_o(n, s, half):
                bank = evac(n, of_tile_before(s, f"OT{half}"))
                nc.scalar.activation(oT[:, 4 * half:4 * half + 4, (1 - s) * P:(2 - s) * P], bank.rearrange("p (j t) -> p j t", j=4),
                                     ACT.Copy).then_inc(tr_evac, 1)

            def evac_wo(n):
                bank = evac(n, "A*WO")
                wait(act, x1_done, n - 1)
                nc.scalar.activation(y1[:], bank[:, 0:2 * P], ACT.Copy).then_inc(tr_evac, 1)

            def evac_ffn_tokens(n):
                bank = evac(n, "B*XT")
                for t in range(2):
                    last = nc.scalar.activation(x_tok[:, t, :], bank[:, t * P:(t + 1) * P], ACT.Identity, accum_out=lmean[:, t:t + 1])
                last.then_inc(tr_evac, 1)

            def centred_squares(n):
                act.wait_ge(ln_done, 2 * n - 1)
                for t in range(2):
                    last = nc.scalar.activation(lsq[:, t, :], x_tok[:, t, :], ACT.Square, bias=nmean[:, t:t + 1], accum_out=lvar[:, t:t + 1])
                last.then_inc(ln_squared, 1)

            def evac_ffn_columns(n):
                bank = evac(n, "B*XN")
                act.wait_ge(ffn_loaded, (n - 1) // PAIRS * 64 + 64)
                nc.scalar.activation(xnT[:], bank[:, 0:2 * P], ACT.Identity, bias=ffn_cols[:, 1:2], scale=ffn_cols[:, 0:1]).then_inc(tr_evac, 1)

            def evac_up(n, j):
                m = FFB[j]
                bank = evac(n, f"B*H{j}")
                wait(act, hidden_done, 3 * (n - 1))
                nc.scalar.activation(gate[0:m, j, :], bank[0:m, 2 * P:4 * P], ACT.Gelu, bias=ffn_cols[0:m, 5 + j:6 + j])
                nc.scalar.activation(up[0:m, j, :], bank[0:m, 0:2 * P], ACT.Identity, bias=ffn_cols[0:m, 2 + j:3 + j]).then_inc(tr_evac, 1)

            def evac_down(n):
                bank = evac(n, "B*FO")
                wait(act, x2_done, n - 1)
                nc.scalar.activation(y2[:], bank[:, 0:2 * P], ACT.Identity, bias=ffn_cols[:, 8:9]).then_inc(tr_evac, 1)

            def turn(n):
                new, old = has_pair(n), has_before(n)
                i = 2 * n
                if new:
                    square(i, 0)
                if old:
                    evac_q(n, 0, 1)
                    evac_k(n, 0, 1)
                if new:
                    square(i, 1)
                if old:
                    evac_p(n, 0, 0)
                    evac_p(n, 0, 1)
                if new:
                    evac_v(i, 0, 0)
                if old:
                    evac_o(n, 0, 0)
                    exps(i - 1, 2)
                if new:
                    square(i, 2)
                if old:
                    exps(i - 1, 3)
                if new:
                    square(i, 3)
                    evac_q(n, 0, 0)
                    evac_k(n, 0, 0)
                if old:
                    evac_p(n, 0, 2)
                    evac_p(n, 0, 3)
                if new:
                    evac_v(i, 0, 1)
                if old:
                    evac_o(n, 0, 1)
                if new:
                    exps(i, 0)
                    exps(i, 1)
                if old:
                    evac_wo(n)
                i = 2 * n + 1
                if new:
                    square(i, 0)
                    square(i, 1)
                    evac_q(n, 1, 1)
                if old:
                    evac_ffn_tokens(n)
                if new:
                    evac_k(n, 1, 1)
                    evac_p(n, 1, 0)
                    evac_v(i, 1, 0)
                if old:
                    centred_squares(n)
                if new:
                    evac_p(n, 1, 1)
                    exps(i - 1, 2)
                    square(i, 2)
                    exps(i - 1, 3)
                    evac_o(n, 1, 0)
                    square(i, 3)
                    evac_v(i, 1, 1)
                    evac_p(n, 1, 2)
                    evac_q(n, 1, 0)
                if old:
                    evac_ffn_columns(n)
                if new:
                    evac_p(n, 1, 3)
                    evac_k(n, 1, 0)
                if old:
                    evac_up(n, 0)
                    evac_up(n, 1)
                    evac_up(n, 2)
                if new:
                    exps(i, 0)
                    evac_o(n, 1, 1)
                if old:
                    evac_down(n)
                if new:
                    exps(i, 1)

            over_turns(act, turn)

        @block.vector
        def _(dve):
            def shift(n, s):
                c = pair_column(n) + s * P
                dve.tensor_scalar(xs[0:64, s, :], xT[0:64, bass.ds(c, P)], 1.0, None, ALU.mult)
                dve.tensor_scalar(xs[64:P, s, :], xT[64:P, bass.ds(c - 1, P)], 1.0, None, ALU.mult).then_inc(xs_done, 1)

            def top_of(i, q):
                dve.wait_ge(s_full, 4 * i + q + 1)
                dve.tensor_reduce(neg_top[:, 4 * q:4 * q + 4], heads4(s_bank(q)), AX_X, ALU.max, negate=True).then_inc(max_done, 1)

            def invert_sum(i, q):
                dve.wait_ge(exp_done, 4 * i + q + 1)
                wait(dve, probs_normed, 4 * (i - 1) + q + 1)
                dve.reciprocal(rtotal[:, 4 * q:4 * q + 4], total[:, 4 * q:4 * q + 4]).then_inc(rec_done, 1)

            def rotate(i, par, c):
                bank = psum[:, c % 2, :].rearrange("p (h d) -> p h d", d=DHEAD)
                t = turn_tables[:, par, :].rearrange("p (f d) -> p f d", f=4)
                cos, sin = t[:, 2 * (c % 2), :], t[:, 2 * (c % 2) + 1, :]
                dve.wait_ge(squared, 4 * i + c + 1)
                if c == 0:
                    dve.wait_ge(tables_done, i + 1)
                wait(dve, (q_normed, k_normed)[c % 2], 2 * (i - 1) + c // 2 + 1)
                straight_c = straight[:, c, :].rearrange("p (h d) -> p h d", d=DHEAD)
                crossed_c = crossed[:, c, :].rearrange("p (h d) -> p h d", d=DHEAD)
                hd = DHEAD // 2
                dve.tensor_tensor(straight_c, bank, cos.unsqueeze(1).broadcast_to([P, 8, DHEAD]), ALU.mult)
                for lo, hi in ((0, hd), (hd, 0)):
                    x = dve.tensor_tensor(crossed_c[:, :, lo:lo + hd], bank[:, :, hi:hi + hd],
                                          sin[:, lo:lo + hd].unsqueeze(1).broadcast_to([P, 8, hd]), ALU.mult)
                x.then_inc(rotary_done, 1)
                wait(dve, newton, STEPS * (2 * (i - 1) + c // 2 + 1))
                dve.tensor_reduce(norm2[:, 8 * c:8 * c + 8], squares[:, c, :].rearrange("p (h d) -> p h d", d=DHEAD),
                                  AX_X, ALU.add).then_inc(norm2_done, 1)

            def norms(i, half):
                dve.wait_ge(norm2_done, 4 * i + 2 * half + 2)
                at = slice(HEADS * half, HEADS * half + HEADS)
                return Rsqrt(dve, newton, STEPS * (2 * i + half), norm2[:, at], norm2c[:, at], rnorm[:, at], na[:, at], nb[:, at])

            def scale_k(i, half):
                c = 2 * half + 1
                dve.wait_ge(newton, STEPS * (2 * i + half + 1))
                dve.wait_ge(qk_added, 4 * i + c + 1)
                dve.tensor_tensor(qk[:, c, :].rearrange("p (h d) -> p h d", d=DHEAD),
                                  straight[:, c, :].rearrange("p (h d) -> p h d", d=DHEAD),
                                  spread(rnorm[:, 8 * c:8 * c + 8], [P, 8, DHEAD]), ALU.mult).then_inc(k_normed, 1)

            def previous_keys(n, s):
                dve.wait_ge(tr_evac, job(n, of_tile_before(s, "KT1")) + 1)
                keep = 1.0 if s == 1 else inside[:, bass.ds(n % (TPB // 2), 1)]
                dve.tensor_scalar(kT[:, s, :, :, 0:WINDOW].rearrange("p j h t -> p (j h) t"),
                                  kT[:, 1 - s, :, :, P:P + WINDOW].rearrange("p j h t -> p (j h) t"), keep, None, ALU.mult).then_inc(kprev_done, 1)

            def begin_residual(n):
                c = pair_column(n - 1)
                dve.wait_ge(wo_begun, n)
                dve.tensor_tensor(x1T[:, bass.ds(c, 2 * P)], psum[:, 2, 0:2 * P], xT[:, bass.ds(c, 2 * P)], ALU.add).then_inc(x1_begun, 1)

            def attention_residual(n):
                c = pair_column(n - 1)
                dve.wait_ge(x1_begun, n)
                dve.wait_ge(tr_evac, job(n, "A*WO") + 1)
                dve.tensor_tensor(x1T[:, bass.ds(c, 2 * P)], y1[:], x1T[:, bass.ds(c, 2 * P)], ALU.add).then_inc(x1_done, 1)

            def shift_pair(n):
                c = pair_column(n - 1)
                dve.wait_ge(x1_done, n)
                dve.tensor_scalar(xs2[0:64, :], x1T[0:64, bass.ds(c, 2 * P)], 1.0, None, ALU.mult)
                dve.tensor_scalar(xs2[64:P, :], x1T[64:P, bass.ds(c - 1, 2 * P)], 1.0, None, ALU.mult).then_inc(xs2_done, 1)

            def layernorm_mean(n):
                dve.wait_ge(tr_evac, job(n, "B*XT") + 1)
                dve.tensor_scalar(nmean[:], lmean[:], -1.0 / DIM, None, ALU.mult).then_inc(ln_done, 1)

            def layernorm_variance(n):
                dve.wait_ge(ln_squared, n)
                dve.tensor_scalar(lvare[:], lvar[:], 1.0 / DIM, 1e-5, ALU.mult, ALU.add).then_inc(ln_done, 1)

            def layernorm_rsqrt(n):
                dve.wait_ge(ln_done, 2 * n)
                return Rsqrt(dve, ln_newton, STEPS * (n - 1), lvare[:], lvarc[:], rstd[:], la[:], lb[:])

            def layernorm_apply(n):
                dve.wait_ge(ln_newton, STEPS * n)
                for t in range(2):
                    last = dve.tensor_scalar(xn_tok[:, t, :], x_tok[:, t, :], nmean[:, t:t + 1], rstd[:, t:t + 1], ALU.add, ALU.mult)
                last.then_inc(xn_done, 1)

            def gated(n, j):
                m = FFB[j]
                dve.wait_ge(tr_evac, job(n, f"B*H{j}") + 1)
                dve.tensor_tensor(hidden[0:m, j, :], up[0:m, j, :], gate[0:m, j, :], ALU.mult).then_inc(hidden_done, 1)

            def ffn_residual(n):
                c = pair_column(n - 1)
                dve.wait_ge(tr_evac, job(n, "B*FO") + 1)
                dve.tensor_tensor(xT[:, bass.ds(c, 2 * P)], y2[:], x1T[:, bass.ds(c, 2 * P)], ALU.add).then_inc(x2_done, 1)

            def turn(n):
                new, old = has_pair(n), has_before(n)
                i = 2 * n
                if old:
                    invert_sum(i - 1, 1)
                if new:
                    rotate(i, 0, 0)
                    rotate(i, 0, 1)
                    roots = norms(i, 0)
                    roots.steps(3)
                if old:
                    top_of(i - 1, 2)
                if new:
                    roots.steps(8)
                if old:
                    top_of(i - 1, 3)
                if new:
                    shift(n, 1)
                if new and old:
                    previous_keys(n, 0)
                if old:
                    invert_sum(i - 1, 2)
                if new:
                    scale_k(i, 0)
                if old:
                    begin_residual(n)
                    invert_sum(i - 1, 3)
                if new:
                    rotate(i, 0, 2)
                    rotate(i, 0, 3)
                    roots = norms(i, 1)
                    roots.steps(1)
                    top_of(i, 0)
                    roots.steps(4)
                    top_of(i, 1)
                    roots.steps(6)
                    invert_sum(i, 0)
                    scale_k(i, 1)
                i = 2 * n + 1
                if new:
                    invert_sum(i - 1, 1)
                if old:
                    attention_residual(n)
                    shift_pair(n)
                if new:
                    rotate(i, 1, 0)
                if old:
                    layernorm_mean(n)
                if new:
                    rotate(i, 1, 1)
                    top_of(i - 1, 2)
                if old:
                    layernorm_variance(n)
                if new:
                    roots = norms(i, 0)
                    roots.steps(1)
                if old:
                    root = layernorm_rsqrt(n)
                    root.steps(1)
                if new:
                    roots.steps(1)
                if old:
                    root.steps(1)
                if new:
                    top_of(i - 1, 3)
                    roots.steps(2)
                if old:
                    root.steps(1)
                if new:
                    roots.steps(1)
                if old:
                    root.steps(1)
                if new:
                    roots.steps(2)
                if old:
                    root.steps(2)
                if new:
                    roots.steps(1)
                    invert_sum(i - 1, 2)
                    roots.steps(3)
                if old:
                    root.steps(3)
                if new:
                    invert_sum(i - 1, 3)
                if old:
                    root.steps(2)
                    layernorm_apply(n)
                if new:
                    scale_k(i, 0)
                    rotate(i, 1, 2)
                    previous_keys(n, 1)
                    rotate(i, 1, 3)
                    roots = norms(i, 1)
                    roots.steps(3)
                if new and has_next(n):
                    shift(n + 1, 0)
                if new:
                    roots.steps(1)
                    top_of(i, 0)
                    roots.steps(1)
                if old:
                    gated(n, 0)
                    gated(n, 1)
                if new:
                    roots.steps(1)
                if old:
                    gated(n, 2)
                if new:
                    roots.steps(3)
                    top_of(i, 1)
                    roots.steps(2)
                    scale_k(i, 1)
                if old:
                    ffn_residual(n)
                if new:
                    invert_sum(i, 0)

            shift(0, 0)
            over_turns(dve, turn)

        @block.gpsimd
        def _(pool):
            def fold(i, n, s):
                pool.wait_ge(scales_loaded, i // TILES * 16 + 16)
                wait(pool, norm2_done, 4 * (i - 1))
                at = (n % (TPB // 2) * 2 + s) * (4 * DHEAD)
                pool.tensor_tensor(turn_tables[:, s, :], tables[:, bass.ds(at, 4 * DHEAD)], qk_scales[:], ALU.mult).then_inc(tables_done, 1)

            def normalise(i, q):
                pool.wait_ge(rec_done, 4 * i + q + 1)
                pool.tensor_tensor(heads4(probs_n[:, q, :]), heads4(probs[:, q, :]),
                                   spread(rtotal[:, 4 * q:4 * q + 4], [P, 4, KEYS]), ALU.mult).then_inc(probs_normed, 1)

            def add(i, c):
                pool.wait_ge(rotary_done, 4 * i + c + 1)
                pool.tensor_tensor(straight[:, c, :], straight[:, c, :], crossed[:, c, :], ALU.add).then_inc(qk_added, 1)

            def scale_q(i, half):
                c = 2 * half
                pool.wait_ge(newton, STEPS * (2 * i + half + 1))
                pool.wait_ge(qk_added, 4 * i + c + 1)
                pool.tensor_tensor(qk[:, c, :].rearrange("p (h d) -> p h d", d=DHEAD),
                                   straight[:, c, :].rearrange("p (h d) -> p h d", d=DHEAD),
                                   spread(rnorm[:, 8 * c:8 * c + 8], [P, 8, DHEAD]), ALU.mult).then_inc(q_normed, 1)

            def turn(n):
                new, old = has_pair(n), has_before(n)
                i = 2 * n
                if old:
                    normalise(i - 1, 1)
                if new:
                    add(i, 0)
                    add(i, 1)
                    scale_q(i, 0)
                if old:
                    normalise(i - 1, 2)
                    normalise(i - 1, 3)
                if new:
                    add(i, 2)
                    fold(i + 1, n, 1)
                    add(i, 3)
                    scale_q(i, 1)
                    normalise(i, 0)
                i = 2 * n + 1
                if new:
                    normalise(i - 1, 1)
                    add(i, 0)
                    add(i, 1)
                if new and has_next(n):
                    fold(i + 1, n + 1, 0)
                if new:
                    normalise(i - 1, 2)
                    scale_q(i, 0)
                    normalise(i - 1, 3)
                    add(i, 2)
                    add(i, 3)
                    scale_q(i, 1)
                    normalise(i, 0)

            fold(0, 0, 0)
            over_turns(pool, turn)


def window_attention(nc, dram, const, base, xT, psum):
    ident, ident16, masks = const["ident"], const["ident16"], const["masks"]
    HD = DIM // HEADS
    BLOCKS = 2 * TILES
    ctx = ExitStack()
    with ctx:
        def sb(n, shape, dt=FP32):
            return ctx.enter_context(nc.sbuf_tensor(f"wa_{n}", shape, dt))

        def sem(n):
            return ctx.enter_context(nc.semaphore(f"wa_{n}"))

        w = sb("w", [P, 4, DIM])
        head_rows = sb("head_rows", [P, HEADS])
        qTall = sb("qTall", [P, TILES * P])
        kTall = sb("kTall", [P, BATCH * PADDED])
        v_win = sb("v_win", [KEYS, BLOCKS, DIM])
        q_heads = sb("q_heads", [P, 2, HEADS, P])
        k_tile = sb("k_tile", [P, 2, WINDOW + P])
        v_tile = sb("v_tile", [KEYS, 2, 2, DIM])
        neg_top = sb("neg_top", [P, HEADS])
        probs = sb("probs", [P, 4, QUAD])
        total, rtotal = sb("total", [P, HEADS]), sb("rtotal", [P, HEADS])
        probs_n = sb("probs_n", [P, 4, QUAD])
        pT = sb("pT", [KEYS, 4, 4 * P])
        o_tok = sb("o_tok", [P, DIM])
        oT = sb("oT", [P, P])

        loaded, kv_full, kv_evac, q_spread = sem("loaded"), sem("kv_full"), sem("kv_evac"), sem("q_spread")
        s_full, max_done, exp_done = sem("s_full"), sem("max_done"), sem("exp_done")
        rec_done, probs_normed = sem("rec_done"), sem("probs_normed")
        p_turned, p_evac, o_full, o_evac = sem("p_turned"), sem("p_evac"), sem("o_full"), sem("o_evac")
        o_turned, oT_evac, y_full, y_added = sem("o_turned"), sem("oT_evac"), sem("y_full"), sem("y_added")
        k_zeroed, k_copied, v_copied = sem("k_zeroed"), sem("k_copied"), sem("v_copied")
        block = ctx.enter_context(nc.Block())

        def s_bank(q):
            return psum[:, q % 2, 0:QUAD]

        GROUPS = 2 * (TILES // 4) + BLOCKS // 4

        def over_steps(eng, step):
            step(0, 0)
            step(1, 1)
            with eng.Fori(1, TILES // 2 - 1) as p:
                step(2 * p, 0)
                step(2 * p + 1, 1)
            step(TILES - 2, 0)
            step(TILES - 1, 1)
            step(TILES, 0)
            step(TILES + 1, 1)

        def scored(t):
            return not isinstance(t, int) or t < TILES

        def another(t):
            return not isinstance(t, int) or t < TILES - 1

        def valued(t):
            return not isinstance(t, int) or 1 <= t <= TILES

        def ended(t):
            return not isinstance(t, int) or t >= 2

        @block.sync
        def _(sp):
            sp.dma_start(w[:], dram["Wattn"].rearrange("f p n -> p f n")).then_inc(loaded, 16)
            sp.dma_start(head_rows[:], dram["head_rows"]).then_inc(loaded, 16)

        @block.tensor
        def _(pe):
            pe.wait_ge(loaded, 32)
            for g in range(GROUPS):
                if g >= 8:
                    pe.wait_ge(kv_evac, g - 7)
                if g < 8:
                    c = pair_column(2 * (g % 4))
                    nc.tensor.matmul(psum[:, g % 8, :], w[:, g // 4, :], xT[:, c:c + 4 * P], start=True, stop=True).then_inc(kv_full, 1)
                else:
                    for j in range(4):
                        b = 4 * (g - 8) + j
                        c = pair_column(b // 4) + b % 4 * 64 - WINDOW
                        last = nc.tensor.matmul(psum[0:KEYS, g % 8, j * P:(j + 1) * P], xT[:, c:c + KEYS], w[:, 2, :],
                                                start=True, stop=True, skip_group_check=True)
                    last.then_inc(kv_full, 1)
            pe.wait_ge(kv_evac, GROUPS)

            def scores(t, s, q):
                wait(pe, exp_done, 4 * t + q - 1)
                if q == 0:
                    pe.wait_ge(q_spread, t + 1)
                    pe.wait_ge(k_copied, t + 1)
                mask = masks[:, bass.ds(t // 2 % (TPB // 2) * QUAD, QUAD)] if s == 0 else masks[:, QUAD:2 * QUAD]
                nc.tensor.matmul(s_bank(q), ident16[:], mask, start=True, stop=False, skip_group_check=True)
                for h in range(4):
                    for b in range(2):
                        last = nc.tensor.matmul(s_bank(q)[64 * b:64 * b + 64, h * KEYS:(h + 1) * KEYS],
                                                q_heads[:, s, 4 * q + h, 64 * b:64 * b + 64],
                                                k_tile[:, s, 64 * b:64 * b + KEYS], start=False, stop=True, skip_group_check=True)
                last.then_inc(s_full, 1)

            def turn_probs(t, q):
                wait(pe, p_evac, 4 * t + q - 1)
                pe.wait_ge(probs_normed, 4 * t + q + 1)
                for h in range(4):
                    last = nc.tensor.transpose(psum[0:KEYS, 2 + q % 2, h * P:(h + 1) * P], probs_n[:, q, h * KEYS:(h + 1) * KEYS], ident[:])
                last.then_inc(p_turned, 1)

            def times_v(t, s):
                wait(pe, o_evac, t)
                pe.wait_ge(p_evac, 4 * t + 4)
                pe.wait_ge(v_copied, t + 1)
                for h in range(HEADS):
                    for b in range(2):
                        last = nc.tensor.matmul(psum[64 * b:64 * b + 64, 4, h * HD:(h + 1) * HD],
                                                pT[:, h // 4, h % 4 * P + 64 * b:h % 4 * P + 64 * b + 64],
                                                v_tile[:, s, b, h * HD:(h + 1) * HD],
                                                start=True, stop=True, skip_group_check=True)
                last.then_inc(o_full, 1)

            def turn_output(t):
                wait(pe, oT_evac, t)
                pe.wait_ge(o_evac, t + 1)
                nc.tensor.transpose(psum[:, 5, 0:P], o_tok[:], ident[:]).then_inc(o_turned, 1)

            def times_wo(t):
                wait(pe, y_added, t)
                pe.wait_ge(oT_evac, t + 1)
                nc.tensor.matmul(psum[:, 6, 0:DIM], oT[:], w[:, 3, :], start=True, stop=True).then_inc(y_full, 1)

            def step(t, s):
                if scored(t):
                    scores(t, s, 0)
                if ended(t):
                    turn_output(t - 2)
                if scored(t):
                    scores(t, s, 1)
                if valued(t):
                    turn_probs(t - 1, 0)
                if ended(t):
                    times_wo(t - 2)
                if valued(t):
                    turn_probs(t - 1, 1)
                if scored(t):
                    scores(t, s, 2)
                if valued(t):
                    turn_probs(t - 1, 2)
                    turn_probs(t - 1, 3)
                if scored(t):
                    scores(t, s, 3)
                if valued(t):
                    times_v(t - 1, 1 - s)

            over_steps(pe, step)

        @block.scalar
        def _(act):
            act.wait_ge(k_zeroed, 1)
            for g in range(GROUPS):
                act.wait_ge(kv_full, g + 1)
                if g < 4:
                    nc.scalar.activation(qTall[:, 4 * P * g:4 * P * (g + 1)], psum[:, g, :], ACT.Copy, scale=1.0 / float(np.sqrt(HD))).then_inc(kv_evac, 1)
                elif g < 8:
                    c = pair_column(2 * (g - 4))
                    nc.scalar.activation(kTall[:, c:c + 4 * P], psum[:, g, :], ACT.Copy).then_inc(kv_evac, 1)
                else:
                    nc.scalar.activation(v_win[:, 4 * (g - 8):4 * (g - 7), :], psum[0:KEYS, g % 8, :].rearrange("p (j d) -> p j d", j=4), ACT.Copy).then_inc(kv_evac, 1)

            def exps(t, q):
                act.wait_ge(max_done, 4 * t + q + 1)
                wait(act, probs_normed, 4 * (t - 1) + q + 1)
                for h in range(4):
                    at, one = slice(h * KEYS, (h + 1) * KEYS), slice(4 * q + h, 4 * q + h + 1)
                    last = nc.scalar.activation(probs[:, q, at], s_bank(q)[:, at], ACT.Exp, bias=neg_top[:, one], accum_out=total[:, one])
                last.then_inc(exp_done, 1)

            def evac_p(t, q):
                act.wait_ge(p_turned, 4 * t + q + 1)
                if q == 0:
                    wait(act, o_full, t)
                nc.scalar.activation(pT[:, q, :], psum[0:KEYS, 2 + q % 2, :], ACT.Copy).then_inc(p_evac, 1)

            def evac_output(t):
                act.wait_ge(o_full, t + 1)
                wait(act, o_turned, t)
                nc.scalar.activation(o_tok[:], psum[:, 4, 0:P], ACT.Copy).then_inc(o_evac, 1)

            def evac_turned(t):
                act.wait_ge(o_turned, t + 1)
                wait(act, y_full, t)
                nc.scalar.activation(oT[:], psum[:, 5, 0:P], ACT.Copy).then_inc(oT_evac, 1)

            def step(t, s):
                if ended(t):
                    evac_turned(t - 2)
                if scored(t):
                    exps(t, 0)
                if valued(t):
                    evac_p(t - 1, 0)
                if scored(t):
                    exps(t, 1)
                if valued(t):
                    for q in range(1, 4):
                        evac_p(t - 1, q)
                if scored(t):
                    exps(t, 2)
                    exps(t, 3)
                if valued(t):
                    evac_output(t - 1)

            over_steps(act, step)

        @block.vector
        def _(dve):
            dve.memset(kTall[:], 0.0).then_inc(k_zeroed, 1)

            def top_of(t, q):
                dve.wait_ge(s_full, 4 * t + q + 1)
                dve.tensor_reduce(neg_top[:, 4 * q:4 * q + 4], heads4(s_bank(q)), AX_X, ALU.max, negate=True).then_inc(max_done, 1)

            def invert_sum(t, q):
                dve.wait_ge(exp_done, 4 * t + q + 1)
                wait(dve, probs_normed, 4 * (t - 1) + q + 1)
                dve.reciprocal(rtotal[:, 4 * q:4 * q + 4], total[:, 4 * q:4 * q + 4]).then_inc(rec_done, 1)

            def spread_q(t, s):
                if isinstance(t, int) and t == 0:
                    dve.wait_ge(loaded, 32)
                    dve.wait_ge(kv_evac, GROUPS)
                wait(dve, s_full, 4 * (t - 1))
                dve.tensor_tensor(q_heads[:, s, :, :], qTall[:, bass.ds(t * P, P)].unsqueeze(1).broadcast_to([P, HEADS, P]),
                                  spread(head_rows[:], [P, HEADS, P]), ALU.mult).then_inc(q_spread, 1)

            def add_output(t):
                dve.wait_ge(y_full, t + 1)
                row = base[:, bass.ds(t, 1), :].rearrange("p o d -> p (o d)")
                dve.tensor_tensor(row, psum[:, 6, 0:DIM], row, ALU.add).then_inc(y_added, 1)

            def step(t, s):
                if scored(t):
                    top_of(t, 0)
                    top_of(t, 1)
                    invert_sum(t, 0)
                if ended(t):
                    add_output(t - 2)
                if scored(t):
                    top_of(t, 2)
                    if another(t):
                        spread_q(t + 1, 1 - s)
                    invert_sum(t, 1)
                    top_of(t, 3)
                    invert_sum(t, 2)
                    invert_sum(t, 3)

            spread_q(0, 0)
            over_steps(dve, step)

        @block.gpsimd
        def _(pool):
            def copy_keys(t, s):
                wait(pool, s_full, 4 * (t - 1))
                pool.tensor_copy(k_tile[:, s, :], kTall[:, bass.ds(pair_column(t // 2) + s * P - WINDOW, WINDOW + P)]).then_inc(k_copied, 1)

            def copy_values(t, s):
                wait(pool, o_full, t - 1)
                pool.tensor_copy(v_tile[:, s, :, :], v_win[:, bass.ds(2 * t, 2), :]).then_inc(v_copied, 1)

            def normalise(t, q):
                pool.wait_ge(rec_done, 4 * t + q + 1)
                wait(pool, p_turned, 4 * (t - 1) + q + 1)
                pool.tensor_tensor(heads4(probs_n[:, q, :]), heads4(probs[:, q, :]),
                                   spread(rtotal[:, 4 * q:4 * q + 4], [P, 4, KEYS]), ALU.mult).then_inc(probs_normed, 1)

            def step(t, s):
                if scored(t):
                    if another(t):
                        copy_keys(t + 1, 1 - s)
                    normalise(t, 0)
                    normalise(t, 1)
                    copy_values(t, s)
                    normalise(t, 2)
                    normalise(t, 3)

            pool.wait_ge(kv_evac, GROUPS)
            copy_keys(0, 0)
            over_steps(pool, step)


def macaron(nc, dram, out):
    ctx = ExitStack()
    with ctx:
        def sb(n, shape, dt=FP32):
            return ctx.enter_context(nc.sbuf_tensor(n, shape, dt))

        base = sb("base", [P, TILES, DIM])
        xT = sb("xT", [P, BATCH * PADDED])
        const = {
            "ident": sb("ident", [P, P]), "ident16": sb("ident16", [P, P], BF16),
            "masks": sb("masks", [P, TPB // 2 * QUAD], BF16), "tables": sb("tables", [P, TPB * 4 * DHEAD]),
            "inside": sb("inside", [P, TPB // 2]),
        }
        psum = ctx.enter_context(nc.psum_tensor("psum", [P, 8, 512], FP32))

        with ExitStack() as load:
            arrived = load.enter_context(nc.semaphore("arrived"))
            cleared = load.enter_context(nc.semaphore("cleared"))
            block = load.enter_context(nc.Block())

            @block.sync
            def _(sp):
                sp.dma_start(base[:], dram["x"].rearrange("t p d -> p t d")).then_inc(arrived, 16)
                for n, t in const.items():
                    sp.dma_start(t[:], dram[n]).then_inc(arrived, 16)
                sp.wait_ge(arrived, 16 * (1 + len(const)))

            @block.vector
            def _(dve):
                dve.memset(xT[:], 0.0).then_inc(cleared, 1)
                dve.wait_ge(cleared, 1)

        stack(nc, dram, const, base, xT, psum, "f1")
        add_half_of_columns(nc, base, xT, const["ident"], psum, "r1")
        layernorm_to_columns(nc, base, xT, const["ident"], psum, "ln2")
        window_attention(nc, dram, const, base, xT, psum)
        stack(nc, dram, const, base, xT, psum, "f2")
        add_half_of_columns(nc, base, xT, const["ident"], psum, "r2")

        with ExitStack() as store:
            stored = store.enter_context(nc.semaphore("stored"))
            block = store.enter_context(nc.Block())

            @block.sync
            def _(sp):
                sp.dma_start(out.rearrange("t p d -> p t d"), base[:]).then_inc(stored, 16)
                sp.wait_ge(stored, 16)


def rotary_constants():
    f = np.float32
    half = np.arange(0, DHEAD, 2, dtype=f)
    inv_freq = (f(1.0) / f(10000.0) ** (half / f(DHEAD))).astype(f)
    t = np.arange(SEQ, dtype=f)
    freqs = (t[:, None] * inv_freq[None, :]).astype(f)
    freqs = np.concatenate([freqs, freqs], -1)
    base_scale = (half + f(0.4 * DHEAD)) / f(1.4 * DHEAD)
    power = (t - SEQ // 2) / f(WINDOW // 2)
    scale = (base_scale[None, :].astype(f) ** power[:, None].astype(f)).astype(f)
    scale = np.concatenate([scale, scale], -1)
    sign = np.where(np.arange(DHEAD) < DHEAD // 2, f(-1), f(1))
    cos, sin = np.cos(freqs), np.sin(freqs) * sign
    inv = f(1.0) / scale
    table = np.stack([cos * scale, sin * scale, cos * inv, sin * inv], 1).astype(f)
    return np.ascontiguousarray(table.reshape(TPB, P, 4 * DHEAD).transpose(1, 0, 2).reshape(P, -1))


def mask_constants():
    q = np.arange(P)[:, None] % 64
    k = np.arange(KEYS)[None, :]
    plain = np.where((k >= q) & (k <= q + WINDOW), 0.0, MASKED)
    start = np.where((np.arange(P)[:, None] < 64) & (k < WINDOW), MASKED, plain)
    rows = [np.tile(start, (1, 4))] + [np.tile(plain, (1, 4))] * (TPB // 2 - 1)
    return np.concatenate(rows, 1)


def kernel(L0_attn_x, L0_attn_Wq, L0_attn_Wk, L0_attn_Wv, L0_attn_Wo, L0_ffn_Wqkv, L0_ffn_q_scale,
           L0_ffn_k_scale, L0_ffn_Wo, L0_ffn_ln_g, L0_ffn_ln_b, L0_ffn_W1, L0_ffn_b1, L0_ffn_W2, L0_ffn_b2):
    import concourse.bacc as bacc
    import ml_dtypes
    from concourse.bass_utils import run_bass_kernel_spmd

    a = lambda x: np.ascontiguousarray(np.asarray(x))
    hd = DHEAD // 2
    qs, ks = a(L0_ffn_q_scale), a(L0_ffn_k_scale)
    swap = lambda s: np.concatenate([s[:, hd:], s[:, :hd]], 1)
    scales = np.concatenate([qs, swap(qs), ks, swap(ks)], 1)
    b1 = a(L0_ffn_b1)
    cols = np.zeros((DEPTH, P, 9), np.float32)
    cols[:, :, 0], cols[:, :, 1], cols[:, :, 8] = a(L0_ffn_ln_g), a(L0_ffn_ln_b), a(L0_ffn_b2)
    for part in range(2):
        for j, m in enumerate(FFB):
            cols[:, :m, 2 + 3 * part + j] = b1[:, part * FF + j * P:part * FF + j * P + m]
    arrays = {
        "x": a(L0_attn_x).reshape(TILES, P, DIM),
        "Wattn": np.stack([a(w).T for w in (L0_attn_Wq, L0_attn_Wk, L0_attn_Wv, L0_attn_Wo)]),
        "Wqkv": a(L0_ffn_Wqkv), "Wo": a(L0_ffn_Wo), "W1": a(L0_ffn_W1), "W2": a(L0_ffn_W2),
        "qk_scales": np.ascontiguousarray(np.broadcast_to(scales[:, None, :], (DEPTH, P, 4 * DHEAD))),
        "ffn_cols": cols,
        "ident": np.eye(P, dtype=np.float32), "ident16": np.eye(P).astype(ml_dtypes.bfloat16),
        "masks": mask_constants().astype(ml_dtypes.bfloat16), "tables": rotary_constants(),
        "inside": np.tile(np.arange(TPB // 2) > 0, (P, 1)).astype(np.float32),
        "head_rows": (np.arange(P)[:, None] // (DIM // HEADS) == np.arange(HEADS)[None, :]).astype(np.float32),
    }
    nc = bacc.Bacc("TRN2", target_bir_lowering=False, num_devices=1)
    dram = {n: nc.dram_tensor(f"in_{n}", v.shape, mybir.dt.from_np(v.dtype), kind="ExternalInput").ap() for n, v in arrays.items()}
    out = nc.dram_tensor("out", (TILES, P, DIM), FP32, kind="ExternalOutput").ap()
    macaron(nc, dram, out)
    r = run_bass_kernel_spmd(nc, [{f"in_{n}": v for n, v in arrays.items()}], core_ids=[0])
    return r.results[0]["out"].reshape(BATCH, SEQ, DIM)
```
